# Optimizing a Trainium2 kernel written in Bass

```python
import numpy as np
import jax
import jax.numpy as jnp

def _softmax(x, axis=-1):
    return jax.nn.softmax(x, axis=axis)

def _gelu(x):
    return jax.nn.gelu(x, approximate=True)

def _silu(x):
    return jax.nn.silu(x)

def _sigmoid(x):
    return jax.nn.sigmoid(x)

def _layernorm(x, axis=-1, eps=1e-05):
    m = jnp.mean(x, axis=axis, keepdims=True)
    v = jnp.var(x, axis=axis, keepdims=True)
    return (x - m) / jnp.sqrt(v + eps)

def _scatter_add(tgt, idx, src, axis=0):
    return tgt.at[idx].add(src)

def _segment_sum(src, seg, n):
    return jax.ops.segment_sum(src, seg, n)
kernel_name = 'mk_sandwich_d1_jaxref_r8_bdc7f3'

def setup_inputs(seed: int=0):
    np.random.seed(seed)
    _w = jnp.asarray

    def _L0_attn_setup():
        import jax, jax.numpy as jnp
        import numpy as np
        B, T, C = (64, 32, 128)
        N_HEAD, HEAD_SIZE, KV_RANK = (16, 64, 128)
        BLOCK_SIZE = 32
        key = jax.random.key(seed)
        ks = jax.random.split(key, 5)
        HD = N_HEAD * HEAD_SIZE

        def init(k, shape):
            fan_in = shape[0]
            bound = 1.0 / np.sqrt(fan_in)
            return jax.random.uniform(k, shape, jnp.float32, -bound, bound)
        return {'x': jax.random.normal(ks[0], (B, T, C), jnp.float32), 'w_kv_down': init(ks[1], (C, KV_RANK)), 'w_kv_up': init(ks[2], (KV_RANK, 2 * HD)), 'w_q': init(ks[3], (C, HD)), 'w_out': init(ks[4], (HD, C))}
    _L0_attn_in = _L0_attn_setup()

    def _L0_ffn_setup():
        import jax, jax.numpy as jnp
        import numpy as np
        B, S, D, F, E = (1, 128, 128, 512, 8)
        EPS = 1e-05

        def _sublayer(xs, g, b, W1e, b1e, W2e, b2e):
            mu = jnp.mean(xs, axis=-1, keepdims=True)
            var = jnp.mean(jnp.square(xs - mu), axis=-1, keepdims=True)
            h = (xs - mu) * jax.lax.rsqrt(var + EPS) * g + b
            return xs + jax.nn.relu(h @ W1e.T + b1e) @ W2e.T + b2e
        key = jax.random.key(seed)
        ks = jax.random.split(key, 4)
        x = jax.random.normal(ks[0], (B, S, D), jnp.float32)
        centroids = jax.random.normal(ks[1], (E, D), jnp.float32) * 0.1
        gamma = jnp.ones((E, D), jnp.float32)
        beta = jnp.zeros((E, D), jnp.float32)
        W1 = jax.random.normal(ks[2], (E, F, D), jnp.float32) * 0.02
        b1 = jnp.zeros((E, F), jnp.float32)
        W2 = jax.random.normal(ks[3], (E, D, F), jnp.float32) * 0.02
        b2 = jnp.zeros((E, D), jnp.float32)
        return {'x': x, 'centroids': centroids, 'gamma': gamma, 'beta': beta, 'W1': W1, 'b1': b1, 'W2': W2, 'b2': b2}
    _L0_ffn_in = _L0_ffn_setup()
    _d = {'L0_attn_x': _L0_attn_in['x'], 'L0_attn_w_kv_down': _L0_attn_in['w_kv_down'], 'L0_attn_w_kv_up': _L0_attn_in['w_kv_up'], 'L0_attn_w_q': _L0_attn_in['w_q'], 'L0_attn_w_out': _L0_attn_in['w_out'], 'L0_ffn_centroids': _L0_ffn_in['centroids'], 'L0_ffn_gamma': _L0_ffn_in['gamma'], 'L0_ffn_beta': _L0_ffn_in['beta'], 'L0_ffn_W1': _L0_ffn_in['W1'], 'L0_ffn_b1': _L0_ffn_in['b1'], 'L0_ffn_W2': _L0_ffn_in['W2'], 'L0_ffn_b2': _L0_ffn_in['b2']}
    _x0 = _d['L0_attn_x']
    _d['L0_attn_x'] = jax.random.normal(jax.random.fold_in(jax.random.key(seed), 1), (32, 256, 128), dtype=_x0.dtype)
    del _x0
    return _d

def reference(L0_attn_x, L0_attn_w_kv_down, L0_attn_w_kv_up, L0_attn_w_q, L0_attn_w_out, L0_ffn_centroids, L0_ffn_gamma, L0_ffn_beta, L0_ffn_W1, L0_ffn_b1, L0_ffn_W2, L0_ffn_b2):

    def _L0_attn_ref(x, w_kv_down, w_kv_up, w_q, w_out):
        import jax, jax.numpy as jnp
        import numpy as np
        B, T, C = (64, 32, 128)
        N_HEAD, HEAD_SIZE, KV_RANK = (16, 64, 128)
        BLOCK_SIZE = 32
        Bx, Tx, Cx = x.shape
        HD = N_HEAD * HEAD_SIZE
        latent_kv = x @ w_kv_down
        kv = latent_kv @ w_kv_up
        k, v = (kv[..., :HD], kv[..., HD:])
        k = k.reshape(Bx, Tx, N_HEAD, HEAD_SIZE)
        v = v.reshape(Bx, Tx, N_HEAD, HEAD_SIZE)
        q = (x @ w_q).reshape(Bx, Tx, N_HEAD, HEAD_SIZE)
        scale = HEAD_SIZE ** (-0.5)
        att = jnp.einsum('bqhd,bkhd->bhqk', q, k) * scale
        causal = jnp.tril(jnp.ones((Tx, Tx), dtype=bool))
        att = jnp.where(causal, att, -jnp.inf)
        att = jax.nn.softmax(att, axis=-1)
        y = jnp.einsum('bhqk,bkhd->bqhd', att, v)
        y = y.reshape(Bx, Tx, HD)
        return y @ w_out

    def _L0_ffn_ref(x, centroids, gamma, beta, W1, b1, W2, b2):
        import jax, jax.numpy as jnp
        import numpy as np
        B, S, D, F, E = (1, 128, 128, 512, 8)
        EPS = 1e-05

        def _sublayer(xs, g, b, W1e, b1e, W2e, b2e):
            mu = jnp.mean(xs, axis=-1, keepdims=True)
            var = jnp.mean(jnp.square(xs - mu), axis=-1, keepdims=True)
            h = (xs - mu) * jax.lax.rsqrt(var + EPS) * g + b
            return xs + jax.nn.relu(h @ W1e.T + b1e) @ W2e.T + b2e
        feats = x.reshape(-1, x.shape[-1])
        scores = jax.lax.stop_gradient(feats @ centroids.T)
        expert = jnp.argmax(scores, axis=1)
        onehot = jax.nn.one_hot(expert, E, dtype=feats.dtype)
        alpha = jax.nn.sigmoid(jnp.sum(feats * centroids[expert], axis=-1, keepdims=True))
        ys = jax.vmap(_sublayer, in_axes=(None, 0, 0, 0, 0, 0, 0))(feats, gamma, beta, W1, b1, W2, b2)
        y = jnp.einsum('te,etd->td', onehot, ys)
        out = alpha * y + (1.0 - alpha) * feats
        return out.reshape(x.shape)
    x = L0_attn_x
    x = x + _layernorm(_L0_attn_ref(_layernorm(x, axis=-1), L0_attn_w_kv_down, L0_attn_w_kv_up, L0_attn_w_q, L0_attn_w_out), axis=-1)
    x = x + _layernorm(_L0_ffn_ref(_layernorm(x, axis=-1), L0_ffn_centroids, L0_ffn_gamma, L0_ffn_beta, L0_ffn_W1, L0_ffn_b1, L0_ffn_W2, L0_ffn_b2), axis=-1)
    return x

_drawn_inputs = setup_inputs


def setup_inputs(seed=0):
    import zlib

    import numpy as np

    out = dict(_drawn_inputs(seed))
    spreads = {'L0_ffn_gamma': (1.0, 0.6),
     'L0_ffn_beta': (0.0, 2.0),
     'L0_ffn_b1': (0.0, 0.755),
     'L0_ffn_b2': (0.0, 0.1)}
    factors = {}
    for name, (base, spread) in spreads.items():
        noise = np.random.default_rng([zlib.crc32(name.encode()), seed]).standard_normal(out[name].shape)
        drawn = base * np.exp(spread * noise) if base else spread * noise
        out[name] = jnp.asarray(drawn.astype(out[name].dtype))
    for name, factor in factors.items():
        out[name] = (out[name] * factor).astype(out[name].dtype)
    return out
```

```python
from contextlib import ExitStack

import concourse.bass as bass
from concourse import mybir

ALU = mybir.AluOpType
ACT = mybir.ActivationFunctionType
AX = mybir.AxisListType
F32 = mybir.dt.float32
F32R = mybir.dt.float32r
BF16 = mybir.dt.bfloat16
U32 = mybir.dt.uint32
I32 = mybir.dt.int32

P = 128
EPS = 1e-5
MASKED = -3.0e38

C_RSTD = 128
C_SHIFT = 129
C_RSTD2 = 130
C_SCORE = 131
C_ID = 132
ROW = 136
NOWHERE = 1 << 20


def block_kernel(nc, x, wd_t, wup, wq_t, wo, cent_t, gamma_t, beta_t, w1_t, b1, w2_t, b2, out):
    ntok, C = x.shape
    T = 256
    NB = ntok // T
    HD = wup.shape[1] // 2
    D = 64
    NH = HD // D
    E = cent_t.shape[1]
    FB = w1_t.shape[2] // P
    PAIRS = NH // 2
    SLOTS = 2 * PAIRS
    ITERS = NB // 2
    REGION = ntok + P
    TILES = ntok // P + E - 1
    TILES += -TILES % 12
    FPAIRS = TILES // 2
    assert C == P and PAIRS == 8 and NB % 2 == 0 and ITERS >= 2

    rows = nc.dram_tensor("routed_rows", [E * REGION + P, ROW], F32, kind="Internal").ap()

    with ExitStack() as ctx:
        def sb(name, shape, dt=F32):
            return ctx.enter_context(nc.sbuf_tensor(name, shape, dt))

        def ps(name, shape, dt=F32):
            return ctx.enter_context(nc.psum_tensor(name, shape, dt))

        def sem(name):
            return ctx.enter_context(nc.semaphore(name))

        psT = ps("psT", [P, 2, T])
        psS = ps("psS", [P, 2, 512])
        psP = ps("psP", [P, 2, 512])
        psZ = ps("psZ", [P, 2, T])
        psU = ps("psU", [P, 512])
        psM = ps("psM", [P, 512])

        ab_hi = sb("ab_hi", [P, NH, 2, P], F32R)
        ab_lo = sb("ab_lo", [P, NH, 2, P], F32R)
        cent = sb("cent", [P, E])
        gam = sb("gam", [P, E])
        bet = sb("bet", [P, E])
        w1g = sb("w1g", [P, E, FB * P + FB])
        w2s = sb("w2s", [P, E, FB, P])
        b2s = sb("b2s", [P, E, P])

        ident = sb("ident", [P, P])
        identb = sb("identb", [P, P], BF16)
        maskb = sb("maskb", [P, P], BF16)
        before = sb("before", [P, P], BF16)
        onesb = sb("onesb", [P, P], BF16)
        neg_half = sb("neg_half", [P, 2])
        eps_t = sb("eps_t", [P, 2])
        rev_e = sb("rev_e", [P, E])
        iota_i = sb("iota_i", [P, E], I32)

        xin = sb("xin", [P, 2, 2, P])
        xres = sb("xres", [P, 2, 2, P])
        st1 = sb("st1", [P, 2, 6])
        mv1 = sb("mv1", [P, 2, 2])
        ve1 = sb("ve1", [P, 2])
        rs1 = sb("rs1", [P, 2])
        xn = sb("xn", [P, 2, P])
        xk_hi = sb("xk_hi", [P, 2, 2, P], F32R)
        xk_lo = sb("xk_lo", [P, 2, 2, P], F32R)
        xt_hi = sb("xt_hi", [P, 2, T], F32R)
        xt_lo = sb("xt_lo", [P, 2, T], F32R)
        t_hi = sb("t_hi", [P, 2, 2, T], F32R)
        t_lo = sb("t_lo", [P, 2, 2, T], F32R)
        nmax = sb("nmax", [P, 4, 2, 2])
        rsum = sb("rsum", [P, 4, 2, 2])
        rinv = sb("rinv", [P, 4, 2, 2])
        prob = sb("prob", [P, 4, 2, 384])
        p_hi = sb("p_hi", [P, 2, 2, 384], F32R)
        p_lo = sb("p_lo", [P, 2, 2, 384], F32R)
        z_hi = sb("z_hi", [P, 2, 2, T], F32R)
        z_lo = sb("z_lo", [P, 2, 2, T], F32R)
        at = sb("at", [P, T])
        st2 = sb("st2", [P, 2, 6])
        mv2 = sb("mv2", [P, 2, 2])
        ve2 = sb("ve2", [P, 2])
        rs2 = sb("rs2", [P, 2])
        an = sb("an", [P, 2, P])
        pay = sb("pay", [P, 2, 2, ROW])
        st3 = sb("st3", [P, 2, 6])
        mv3 = sb("mv3", [P, 2, 2])
        ve3 = sb("ve3", [P, 2])
        w3 = sb("w3", [P, 3, 2])
        fn = sb("fn", [P, 2, P])
        ft = sb("ft", [P, T])
        hits = sb("hits", [P, 2, E])
        hitr = sb("hitr", [P, 2, E])
        first = sb("first", [P, 2])
        oh = sb("oh", [P, 2, E], BF16)
        base = sb("base", [P, 2, E])
        dsum = sb("dsum", [P, 2, E])
        dsel = sb("dsel", [P, 2, E])
        dstf = sb("dstf", [P, 2])
        dst = sb("dst", [P, 2, 2], U32)
        idf = sb("idf", [P, 2, 2])

        wd_s = sb("wd_s", [P, P])
        wup_s = sb("wup_s", [P, 2 * HD])
        wq_s = sb("wq_s", [P, HD // P, P])
        wo_s = sb("wo_s", [P, HD // P, P])
        kv_t = sb("kv_t", [P, 2, HD // P, P])

        names = """w_loaded ffnw_loaded consts_ready kv_done kv_copied ab_done ab_hi_done ab_split bias_done bias_copied
            x_loaded xr_loaded st1_done mv1_done ve1_done rs1_done xn_ready xk_hi_done xn_tr xt_hi_done x_split
            t_ready t_hi_done t_split s_ready nmax_ready probs_ready rinv_ready norm_ready pt_ready p_hi_done p_split
            z_ready z_hi_done z_split u_done u_copied a_tr st2_done mv2_done ve2_done rs2_done a_norm x1_ready
            st3_done mv3_done r3_steps f_ready f_tr ft_ready scored argmax_steps onehot_ready ranked dest_steps
            dest_ready scattered"""
        S = {n: sem(n) for n in names.split()}
        FU = 6
        W1W = FB * P + FB
        regb = sb("regb", [P, E])
        pidx = sb("pidx", [P, 1])
        padr = sb("padr", [P, ROW])
        paddst = sb("paddst", [P, E], U32)
        cnt = sb("cnt", [P, E])
        cnti = sb("cnti", [P, 2, E], I32)
        ntile = sb("ntile", [P, E])
        csum = sb("csum", [P, 4, E])
        tix = sb("tix", [P, TILES])
        tixi = sb("tixi", [P, TILES], I32)
        past = sb("past", [P, TILES, E])
        pastn = sb("pastn", [P, TILES, E])
        texp = sb("texp", [P, TILES])
        tpre = sb("tpre", [P, TILES])
        trow = sb("trow", [P, 3, TILES])
        table = sb("table", [P, TILES, 2], I32)
        fin = sb("fin", [P, FU, 2, ROW])
        ff = sb("ff", [P, FU, 2, P])
        nn = sb("nn", [P, 2, P])
        nt = sb("nt", [P, 2, T])
        w1st = sb("w1st", [P, 2, 2, W1W])
        hid = sb("hid", [P, 2, 2, FB, P])
        ea = sb("ea", [P, FU, 2])
        ea1 = sb("ea1", [P, FU, 2])
        alpha = sb("alpha", [P, FU, 2])
        y3 = sb("y3", [P, 2, P])
        gg = sb("gg", [P, 2, 2, P])
        gst = sb("gst", [P, 2, 6])
        carry = sb("carry", [P, 1])
        gmv = sb("gmv", [P, 2, 2, 2])
        gve = sb("gve", [P, 2])
        grs = sb("grs", [P, 2, 2])
        on = sb("on", [P, 2, P])
        res = sb("res", [P, 2, 2, P])
        for n in """pads_ready pad_stored spare_stored pad_dst_ready table_steps table_ready w1st_ready exp_done nt_ready
            relu_a relu_d ff_done nn_ready n_tr h_done y_done alpha_steps y3_done g_steps gmv_ready gve_done
            grs_ready on_ready res_ready""".split():
            S[n] = sem(n)
        f_loaded = [sem(f"f_loaded{i}") for i in range(FU)]
        stored = [sem(f"stored{i}") for i in range(FU)]
        psH, psN, psY = psS, psU, (psT, psZ)

        def ffn_phases(eng, slot):
            for s in range(FU):
                slot(0, 0, s, lambda lag: s >= lag)
            with eng.Fori(1, FPAIRS // FU) as it:
                m0 = eng.snap(it * FU)
                n0 = eng.snap(it * 32)
                for s in range(FU):
                    slot(m0, n0, s, lambda lag: True)
            for s in range(4):
                slot(FPAIRS, FPAIRS // FU * 32, s, lambda lag: s < lag)

        def expert_of(eng, m, t):
            return eng.value_load(table[0:1, bass.ds(m * 2 + t, 1), 1], min_val=0, max_val=E - 1)

        def ffn_sp(sp):
            sp.wait_ge(S["table_ready"], 1)
            sp.wait_ge(S["scattered"], 32 * NB)
            sp.wait_ge(S["pad_stored"], 16 * E)
            sp.wait_ge(S["spare_stored"], 16)

            def slot(m0, n0, s, live):
                if not live(0):
                    return
                if live(FU):
                    sp.wait_ge(stored[s], n0)
                for t in range(2):
                    row = sp.value_load(table[0:1, bass.ds((m0 + s) * 2 + t, 1), 0], min_val=0, max_val=E * REGION)
                    sp.dma_start(fin[:, s, t, :], rows[bass.ds(row, P), :]).then_inc(f_loaded[s], 16)

            ffn_phases(sp, slot)

        def ffn_pe(pe):
            mm = nc.tensor.matmul
            pe.wait_ge(S["table_ready"], 1)

            def slot(m0, n0, s, live):
                if live(0):
                    pe.wait_ge(S["nn_ready"], m0 + s + 1)
                    if live(1):
                        pe.wait_ge(S["nt_ready"], m0 + s)
                    for t in range(2):
                        last = nc.tensor.transpose(psN[:, t * P:(t + 1) * P], nn[:, t, :], ident[:])
                    last.then_inc(S["n_tr"], 1)
                if live(1):
                    b = (s - 1) % 2
                    pe.wait_ge(S["nt_ready"], m0 + s)
                    pe.wait_ge(S["w1st_ready"], m0 + s)
                    if live(2):
                        pe.wait_ge(S["relu_a"], m0 + s - 1)
                        pe.wait_ge(S["relu_d"], m0 + s - 1)
                    for t in range(2):
                        for j in range(FB):
                            last = mm(psH[:, t, j * P:(j + 1) * P], w1st[:, b, t, j * P:(j + 1) * P],
                                      nt[:, b, t * P:(t + 1) * P], start=True, stop=True)
                    last.then_inc(S["h_done"], 1)
                if live(2):
                    b = (s - 2) % 2
                    pe.wait_ge(S["relu_a"], m0 + s - 1)
                    pe.wait_ge(S["relu_d"], m0 + s - 1)
                    if live(4):
                        pe.wait_ge(S["y3_done"], m0 + s - 3)
                    for t in range(2):
                        e = expert_of(pe, m0 + s - 2, t)
                        for j in range(FB):
                            w2 = w2s[:, bass.ds(e, 1), j, :].rearrange("p a c -> p (a c)")
                            last = mm(psY[b][:, t, 0:P], hid[:, b, t, j, :], w2, start=(j == 0), stop=(j == FB - 1))
                    last.then_inc(S["y_done"], 1)

            ffn_phases(pe, slot)

        def ffn_act(act):
            act.wait_ge(S["table_ready"], 1)

            def slot(m0, n0, s, live):
                if live(0):
                    if live(2):
                        act.wait_ge(S["h_done"], m0 + s - 1)
                        act.wait_ge(S["relu_a"], m0 + s - 1)
                        act.wait_ge(S["relu_d"], m0 + s - 1)
                    for t in range(2):
                        e = expert_of(act, m0 + s, t)
                        last = nc.scalar.activation(w1st[:, s % 2, t, :],
                                                    w1g[:, bass.ds(e, 1), :].rearrange("p a c -> p (a c)"), ACT.Copy)
                    last.then_inc(S["w1st_ready"], 1)
                    act.wait_ge(f_loaded[s], n0 + 32)
                    nc.scalar.activation(ea[:, s, :], fin[:, s, :, C_SCORE], ACT.Exp, scale=-1.0).then_inc(S["exp_done"], 1)
                if live(1):
                    b = (s - 1) % 2
                    act.wait_ge(S["h_done"], m0 + s)
                    if live(3):
                        act.wait_ge(S["y_done"], m0 + s - 2)
                    for j in range(FB):
                        last = nc.scalar.activation(hid[:, b, 0, j, :], psH[:, 0, j * P:(j + 1) * P], ACT.Relu,
                                                    bias=w1st[:, b, 0, FB * P + j:FB * P + j + 1])
                    last.then_inc(S["relu_a"], 1)
                if live(0):
                    act.wait_ge(S["n_tr"], m0 + s + 1)
                    nc.scalar.activation(nt[:, s % 2, :], psN[:, 0:T], ACT.Copy).then_inc(S["nt_ready"], 1)

            ffn_phases(act, slot)

        def ffn_dve(dve):
            v = nc.vector
            k = [0]

            def link(ins):
                k[0] += 1
                ins.then_inc(S["table_steps"], 1)
                dve.wait_ge(S["table_steps"], k[0])

            dve.wait_ge(S["dest_ready"], NB)
            last_base = base[:, NB % 2, :]
            v.tensor_scalar(paddst[:], last_base, pidx[:, 0:1], None, ALU.add).then_inc(S["pad_dst_ready"], 1)
            link(v.tensor_tensor(cnt[:], last_base, regb[:], ALU.subtract))
            link(v.tensor_scalar(cnti[:, 0, :], cnt[:], float(P - 1), None, ALU.add))
            link(v.tensor_single_scalar(cnti[:, 1, :], cnti[:, 0, :], 7, ALU.arith_shift_right))
            link(v.tensor_copy(ntile[:], cnti[:, 1, :]))
            src = ntile[:]
            for n, d in enumerate((1, 2, 4)):
                v.tensor_copy(csum[:, n, 0:d], src[:, 0:d])
                link(v.tensor_tensor(csum[:, n, d:E], src[:, d:E], src[:, 0:E - d], ALU.add))
                src = csum[:, n, :]
            link(v.tensor_tensor(past[:], tix[:].unsqueeze(2).broadcast_to([P, TILES, E]),
                                 src.unsqueeze(1).broadcast_to([P, TILES, E]), ALU.is_ge))
            v.tensor_reduce(texp[:], past[:], AX.X, ALU.add)
            link(v.tensor_tensor(pastn[:], past[:], ntile[:].unsqueeze(1).broadcast_to([P, TILES, E]), ALU.mult))
            link(v.tensor_reduce(tpre[:], pastn[:], AX.X, ALU.add))
            link(v.tensor_tensor(trow[:, 0, :], tix[:], tpre[:], ALU.subtract))
            link(v.tensor_scalar(trow[:, 1, :], trow[:, 0, :], float(P), None, ALU.mult))
            link(v.scalar_tensor_tensor(trow[:, 2, :], texp[:], float(REGION), trow[:, 1, :], ALU.mult, ALU.add))
            v.tensor_scalar(table[:, :, 0], trow[:, 2, :], float(E * REGION), None, ALU.min)
            v.tensor_scalar(table[:, :, 1], texp[:], float(E - 1), None, ALU.min).then_inc(S["table_ready"], 1)
            dve.wait_ge(S["table_ready"], 1)

            def slot(m0, n0, s, live):
                if live(0):
                    dve.wait_ge(f_loaded[s], n0 + 32)
                    for t in range(2):
                        last = v.tensor_scalar(ff[:, s, t, :], fin[:, s, t, 0:P], fin[:, s, t, C_RSTD:C_RSTD + 1],
                                               fin[:, s, t, C_SHIFT:C_SHIFT + 1], ALU.mult, ALU.add)
                    last.then_inc(S["ff_done"], 1)
                    dve.wait_ge(S["ff_done"], m0 + s + 1)
                    if live(1):
                        dve.wait_ge(S["n_tr"], m0 + s)
                    for t in range(2):
                        last = v.tensor_scalar(nn[:, t, :], ff[:, s, t, :], fin[:, s, t, C_RSTD2:C_RSTD2 + 1], None,
                                               ALU.mult)
                    last.then_inc(S["nn_ready"], 1)
                    dve.wait_ge(S["exp_done"], m0 + s + 1)
                    v.tensor_scalar(ea1[:, s, :], ea[:, s, :], 1.0, None, ALU.add).then_inc(S["alpha_steps"], 1)
                    dve.wait_ge(S["alpha_steps"], m0 + s + 1)
                    v.reciprocal(alpha[:, s, :], ea1[:, s, :])
                if live(3):
                    m = (s - 3) % 2
                    dve.wait_ge(S["grs_ready"], m0 + s - 2)
                    if live(4):
                        dve.wait_ge(S["res_ready"], m0 + s - 3)
                    for t in range(2):
                        last = v.tensor_scalar(on[:, t, :], gg[:, m, t, :], gmv[:, m, t, 0:1], grs[:, m, t:t + 1],
                                               ALU.subtract, ALU.mult)
                    last.then_inc(S["on_ready"], 1)
                if live(1):
                    b = (s - 1) % 2
                    dve.wait_ge(S["h_done"], m0 + s)
                    if live(3):
                        dve.wait_ge(S["y_done"], m0 + s - 2)
                    for j in range(FB):
                        last = v.tensor_scalar(hid[:, b, 1, j, :], psH[:, 1, j * P:(j + 1) * P],
                                               w1st[:, b, 1, FB * P + j:FB * P + j + 1], 0.0, ALU.add, ALU.max)
                    last.then_inc(S["relu_d"], 1)
                if live(2):
                    b, sf = (s - 2) % 2, (s - 2) % FU
                    m = m0 + s - 2
                    dve.wait_ge(S["y_done"], m + 1)
                    for t in range(2):
                        e = expert_of(dve, m, t)
                        last = v.tensor_tensor(y3[:, t, :], psY[b][:, t, 0:P],
                                               b2s[:, bass.ds(e, 1), :].rearrange("p a c -> p (a c)"), ALU.add)
                    last.then_inc(S["y3_done"], 1)
                    dve.wait_ge(S["y3_done"], m + 1)
                    for t in range(2):
                        last = v.scalar_tensor_tensor(gg[:, b, t, :], y3[:, t, :], alpha[:, sf, t:t + 1],
                                                      ff[:, sf, t, :], ALU.mult, ALU.add)
                    last.then_inc(S["g_steps"], 1)
                    dve.wait_ge(S["g_steps"], 2 * m + 1)
                    for t in range(2):
                        last = v.bn_stats(gst[:, t, :], gg[:, b, t, :])
                    last.then_inc(S["g_steps"], 1)
                    dve.wait_ge(S["g_steps"], 2 * m + 2)
                    v.tensor_copy(carry[:], gst[:, 0, 0:1])
                    for t in range(2):
                        last = v.bn_aggr(gmv[:, b, t, :], gst[:, t, :])
                    last.then_inc(S["gmv_ready"], 1)

            ffn_phases(dve, slot)

        def ffn_pool(pool):
            g = nc.gpsimd
            pool.wait_ge(S["pads_ready"], 1)
            pool.wait_ge(S["pad_dst_ready"], 1)
            for e in range(E):
                g.indirect_dma_start(rows, bass.IndirectOffsetOnAxis(ap=paddst[:, e:e + 1], axis=0),
                                     padr[:], None).then_inc(S["pad_stored"], 16)

            def slot(m0, n0, s, live):
                if live(2):
                    m, b = m0 + s - 2, (s - 2) % 2
                    pool.wait_ge(S["gmv_ready"], m + 1)
                    g.tensor_tensor(gve[:], gmv[:, b, :, 1], eps_t[:], ALU.add).then_inc(S["gve_done"], 1)
                    pool.wait_ge(S["gve_done"], m + 1)
                    g.tensor_tensor(grs[:, b, :], gve[:], neg_half[:], ALU.pow).then_inc(S["grs_ready"], 1)
                if live(3):
                    m, b, sf = m0 + s - 3, (s - 3) % 2, (s - 3) % FU
                    pool.wait_ge(S["on_ready"], m + 1)
                    if live(5):
                        pool.wait_ge(stored[(s - 5) % FU], n0 + (32 if s >= 5 else 0))
                    g.tensor_tensor(res[:, b], on[:], fin[:, sf, :, 0:P], ALU.add).then_inc(S["res_ready"], 1)
                    wait_apart(pool, S["res_ready"], m + 1)
                    for t in range(2):
                        g.indirect_dma_start(out, bass.IndirectOffsetOnAxis(
                            ap=fin[:, sf, t, C_ID:C_ID + 1].bitcast(U32), axis=0), res[:, b, t, :], None,
                            bounds_check=ntok - 1, oob_is_err=False).then_inc(stored[sf], 16)

            ffn_phases(pool, slot)
            for i in range(FU):
                pool.wait_ge(stored[i], FPAIRS // FU * 32)

        FFN = {"sp": ffn_sp, "pe": ffn_pe, "act": ffn_act, "dve": ffn_dve, "pool": ffn_pool}
        block = ctx.enter_context(nc.Block())

        def wait_apart(eng, what, value):
            eng.wait_ge(S["x_loaded"], 16)
            eng.wait_ge(what, value)

        def phases(eng, slot):
            for s in range(SLOTS):
                slot(0, 0, s, lambda lag: s >= lag, lambda d: s // PAIRS >= d)
            if ITERS > 2:
                with eng.Fori(1, ITERS - 1) as it:
                    g0 = eng.snap(it * SLOTS)
                    b0 = eng.snap(it * 2)
                    for s in range(SLOTS):
                        slot(g0, b0, s, lambda lag: True, lambda d: True)
            for s in range(SLOTS):
                slot((ITERS - 1) * SLOTS, NB - 2, s, lambda lag: True,
                     lambda d: s // PAIRS - d < 2)
            for s in range(SLOTS):
                slot(ITERS * SLOTS, NB, s, lambda lag: s < lag, lambda d: s // PAIRS < d)

        @block.sync
        def _(sp):
            for dst_, src in ((wd_s[:], wd_t), (wup_s[:], wup), (wq_s[:], wq_t), (wo_s[:], wo)):
                sp.dma_start(dst_, src).then_inc(S["w_loaded"], 16)

            def load_x(buf, bpar, b, done):
                src = x[bass.ds(b * T, T), :].rearrange("(t p) c -> p t c", p=P)
                sp.dma_start(buf[:, bpar], src).then_inc(done, 16)

            load_x(xin, 0, 0, S["x_loaded"])
            for dst_, src in ((cent[:], cent_t), (gam[:], gamma_t), (bet[:], beta_t), (w1g[:, :, 0:FB * P], w1_t),
                              (w1g[:, :, FB * P:FB * P + FB], b1), (w2s[:], w2_t),
                              (b2s[:], b2.unsqueeze(0).broadcast_to([P, E, P]))):
                sp.dma_start(dst_, src).then_inc(S["ffnw_loaded"], 16)

            def slot(g0, b0, s, live, live_b):
                r, db = s % PAIRS, s // PAIRS
                if r == 0 and live_b(-1):
                    sp.wait_ge(S["xn_ready"], b0 + db + 1)
                    load_x(xin, (db + 1) % 2, b0 + db + 1, S["x_loaded"])
                if r == 3 and live_b(1):
                    if live_b(2):
                        sp.wait_ge(S["x1_ready"], b0 + db - 1)
                    load_x(xres, (db - 1) % 2, b0 + db - 1, S["xr_loaded"])

            sp.wait_ge(S["pads_ready"], 1)
            sp.dma_start(rows[E * REGION:E * REGION + P, :], padr[:]).then_inc(S["spare_stored"], 16)
            phases(sp, slot)
            FFN["sp"](sp)

        @block.tensor
        def _(pe):
            mm = nc.tensor.matmul
            pe.wait_ge(S["w_loaded"], 64)
            for j in range(HD // P):
                if j >= 2:
                    pe.wait_ge(S["kv_copied"], j - 1)
                for kv in range(2):
                    last = mm(psS[:, j % 2, kv * P:(kv + 1) * P],
                              wup_s[:, kv * HD + j * P:kv * HD + (j + 1) * P], wd_s[:], start=True, stop=True)
                last.then_inc(S["kv_done"], 1)
            for j in range(HD // P):
                pe.wait_ge(S["kv_copied"], j + 1)
                if j >= 1:
                    pe.wait_ge(S["ab_split"], j)
                for e in range(2):
                    h = slice(64 * e, 64 * e + 64)
                    mm(psP[:, e, 0:P], wq_s[h, j, :], kv_t[h, 0, j, :], start=True, stop=True)
                    last = mm(psP[:, e, P:2 * P], kv_t[h, 1, j, :], wo_s[h, j, :], start=True, stop=True)
                last.then_inc(S["ab_done"], 1)
            pe.wait_ge(S["ffnw_loaded"], 7 * 16)
            for e in range(E):
                for j in range(FB):
                    last = mm(psU[:, e * FB + j:e * FB + j + 1], w1g[:, e, j * P:(j + 1) * P], bet[:, e:e + 1],
                              start=True, stop=True)
            last.then_inc(S["bias_done"], 1)

            def turn_x():
                for t in range(2):
                    last = nc.tensor.transpose(psM[:, t * P:(t + 1) * P], xn[:, t, :], ident[:])
                last.then_inc(S["xn_tr"], 1)

            pe.wait_ge(S["consts_ready"], 1)
            pe.wait_ge(S["xn_ready"], 1)
            turn_x()

            def scores(h, tb, xb, freed):
                pe.wait_ge(S["probs_ready"], freed) if freed is not None else None
                diag = psS[:, h, 0:512].rearrange("p (a k) -> p a k", a=2)[:, :, 0:P]
                mm(diag, identb[:], maskb[:].unsqueeze(1).broadcast_to([P, 2, P]),
                   start=True, stop=False, skip_group_check=True)
                for tt, xx in ((t_lo, xt_hi), (t_hi, xt_lo), (t_hi, xt_hi)):
                    last = mm(psS[:, h, 0:P], tt[:, tb, h, 0:P], xx[:, xb, 0:P],
                              start=False, stop=False, skip_group_check=True)
                    last = mm(psS[:, h, P:384], tt[:, tb, h, P:T], xx[:, xb, :],
                              start=False, stop=xx is xt_hi and tt is t_hi, skip_group_check=True)
                last.then_inc(S["s_ready"], 1)

            def slot(g0, b0, s, live, live_b):
                r, db = s % PAIRS, s // PAIRS
                if live(0):
                    if r == 0:
                        pe.wait_ge(S["x_split"], b0 + db + 1)
                    if live(1):
                        pe.wait_ge(S["t_split"], g0 + s)
                    else:
                        pe.wait_ge(S["ab_split"], HD // P)
                    for h in range(2):
                        hh = 2 * r + h
                        mm(psT[:, h, :], ab_lo[:, hh, 0, :], xt_hi[:, db, :], start=True, stop=False)
                        mm(psT[:, h, :], ab_hi[:, hh, 0, :], xt_lo[:, db, :], start=False, stop=False)
                        last = mm(psT[:, h, :], ab_hi[:, hh, 0, :], xt_hi[:, db, :], start=False, stop=True)
                    last.then_inc(S["t_ready"], 1)
                if live(3):
                    p3 = (s - 3) % 4
                    pe.wait_ge(S["norm_ready"], g0 + s - 2)
                    if live(4):
                        pe.wait_ge(S["p_split"], g0 + s - 3)
                    for h in range(2):
                        for k in range(3):
                            last = nc.tensor.transpose(psP[:, h, k * P:(k + 1) * P],
                                                       prob[:, p3, h, k * P:(k + 1) * P], ident[:])
                    last.then_inc(S["pt_ready"], 1)
                if live(1):
                    pe.wait_ge(S["t_split"], g0 + s)
                    xb = ((s - 1) // PAIRS) % 2
                    for h in range(2):
                        scores(h, (s - 1) % 2, xb, 2 * (g0 + s - 2) + 1 + h if live(2) else None)
                if live(4):
                    zb, zx = (s - 4) % 2, ((s - 4) // PAIRS) % 2
                    pe.wait_ge(S["p_split"], g0 + s - 3)
                    if live(5):
                        pe.wait_ge(S["z_split"], g0 + s - 4)
                    terms = ((xk_lo, p_hi), (xk_hi, p_lo), (xk_hi, p_hi))
                    for n, (xx, pp) in enumerate(terms):
                        mm(psZ[:, :, :], xx[:, zx, 0, :], pp[:, zb, :, 0:T], start=(n == 0), stop=False,
                           skip_group_check=True)
                    for n, (xx, pp) in enumerate(terms):
                        last = mm(psZ[:, :, P:T], xx[:, zx, 1, :], pp[:, zb, :, T:384], start=False, stop=(n == 2),
                                  skip_group_check=True)
                    last.then_inc(S["z_ready"], 1)
                if live(5):
                    ub, ur = (s - 5) % 2, (s - 5) % PAIRS
                    pe.wait_ge(S["z_split"], g0 + s - 4)
                    if ur == 0 and live(5 + PAIRS):
                        pe.wait_ge(S["u_copied"], b0 + (s - 5) // PAIRS)
                    for h in range(2):
                        hh = 2 * ur + h
                        for n, (bb, zz) in enumerate(((ab_lo, z_hi), (ab_hi, z_lo), (ab_hi, z_hi))):
                            last = mm(psU[:, 0:T], bb[:, hh, 1, :], zz[:, ub, h, :],
                                      start=(ur == 0 and h == 0 and n == 0),
                                      stop=(ur == PAIRS - 1 and h == 1 and n == 2))
                    last.then_inc(S["u_done"], 1)
                if r == 2 and live_b(2):
                    pe.wait_ge(S["f_ready"], b0 + db - 1)
                    for t in range(2):
                        last = nc.tensor.transpose(psM[:, t * P:(t + 1) * P], fn[:, t, :], ident[:])
                    last.then_inc(S["f_tr"], 1)
                if r == 3 and live_b(2):
                    pe.wait_ge(S["ft_ready"], b0 + db - 1)
                    for t in range(2):
                        last = mm(psM[:, t * E:(t + 1) * E], ft[:, t * P:(t + 1) * P], cent[:], start=True, stop=True)
                    last.then_inc(S["scored"], 1)
                if r == 4 and live_b(2):
                    pe.wait_ge(S["onehot_ready"], b0 + db - 1)
                    mm(psM[:, 0:E], before[:], oh[:, 0, :], start=True, stop=True)
                    mm(psM[:, E:2 * E], before[:], oh[:, 1, :], start=True, stop=False)
                    mm(psM[:, E:2 * E], onesb[:], oh[:, 0, :], start=False, stop=True)
                    mm(psM[:, 2 * E:3 * E], onesb[:], oh[:, 0, :], start=True, stop=False)
                    mm(psM[:, 2 * E:3 * E], onesb[:], oh[:, 1, :], start=False, stop=True).then_inc(S["ranked"], 1)
                if r == 5 and live_b(-1):
                    pe.wait_ge(S["xn_ready"], b0 + db + 2)
                    if live_b(2):
                        pe.wait_ge(S["dest_ready"], b0 + db - 1)
                    turn_x()
                if r == 6 and live_b(1):
                    pe.wait_ge(S["u_copied"], b0 + db)
                    if live_b(-1):
                        pe.wait_ge(S["x_split"], b0 + db + 2)
                    elif live_b(2):
                        pe.wait_ge(S["dest_ready"], b0 + db - 1)
                    for t in range(2):
                        last = nc.tensor.transpose(psM[:, t * P:(t + 1) * P], at[:, t * P:(t + 1) * P], ident[:])
                    last.then_inc(S["a_tr"], 1)

            phases(pe, slot)
            FFN["pe"](pe)

        @block.scalar
        def _(act):
            cp = lambda o, i: nc.scalar.activation(o, i, ACT.Copy)
            for j in range(HD // P):
                act.wait_ge(S["kv_done"], j + 1)
                nc.scalar.activation(kv_t[:, 0, j, :], psS[:, j % 2, 0:P], ACT.Copy, scale=float(D) ** -0.5)
                cp(kv_t[:, 1, j, :], psS[:, j % 2, P:2 * P]).then_inc(S["kv_copied"], 1)
            for j in range(HD // P):
                act.wait_ge(S["ab_done"], j + 1)
                cp(ab_hi[:, 2 * j:2 * j + 2].rearrange("p h m c -> p h (m c)"),
                   psP[:, :, 0:2 * P]).then_inc(S["ab_hi_done"], 1)

            def xt_top(par):
                cp(xt_hi[:, par, :], psM[:, 0:T]).then_inc(S["xt_hi_done"], 1)

            act.wait_ge(S["xn_tr"], 1)
            xt_top(0)

            def slot(g0, b0, s, live, live_b):
                r, db = s % PAIRS, s // PAIRS
                if live(0):
                    act.wait_ge(S["t_ready"], g0 + s + 1)
                    if live(2):
                        act.wait_ge(S["s_ready"], 2 * (g0 + s - 1))
                    cp(t_hi[:, s % 2], psT[:]).then_inc(S["t_hi_done"], 1)
                if r == 3 and live_b(2):
                    act.wait_ge(S["f_tr"], b0 + db - 1)
                    cp(ft[:], psM[:, 0:T]).then_inc(S["ft_ready"], 1)
                if r == 5 and live_b(1):
                    act.wait_ge(S["u_done"], PAIRS * (b0 + db))
                    if live_b(2):
                        act.wait_ge(S["a_tr"], b0 + db - 1)
                    cp(at[:], psU[:, 0:T]).then_inc(S["u_copied"], 1)
                if r == 6 and live_b(-1):
                    act.wait_ge(S["xn_tr"], b0 + db + 2)
                    if live_b(1):
                        act.wait_ge(S["s_ready"], 2 * PAIRS * (b0 + db))
                    xt_top((db + 1) % 2)
                if live(3):
                    act.wait_ge(S["pt_ready"], g0 + s - 2)
                    if live(5):
                        act.wait_ge(S["z_ready"], g0 + s - 4)
                    cp(p_hi[:, (s - 3) % 2], psP[:, :, 0:384]).then_inc(S["p_hi_done"], 1)
                if live(1):
                    p1 = (s - 1) % 4
                    for h in range(2):
                        act.wait_ge(S["nmax_ready"], 2 * (g0 + s - 1) + 1 + h)
                        for q, (a, z) in enumerate(((0, P), (P, 384))):
                            last = nc.scalar.activation(prob[:, p1, h, a:z], psS[:, h, a:z], ACT.Exp,
                                                        bias=nmax[:, p1, h, q:q + 1],
                                                        accum_out=rsum[:, p1, h, q:q + 1])
                        last.then_inc(S["probs_ready"], 1)
                if live(4):
                    act.wait_ge(S["z_ready"], g0 + s - 3)
                    if live(6):
                        act.wait_ge(S["u_done"], g0 + s - 5)
                    cp(z_hi[:, (s - 4) % 2], psZ[:]).then_inc(S["z_hi_done"], 1)

            phases(act, slot)
            FFN["act"](act)

        @block.vector
        def _(dve):
            v = nc.vector

            def stats(src, st, mv, st_done, mv_done, n):
                for t in range(2):
                    last = v.bn_stats(st[:, t, :], src(t))
                last.then_inc(st_done, 1)
                wait_apart(dve, st_done, n)
                for t in range(2):
                    last = v.bn_aggr(mv[:, t, :], st[:, t, :])
                last.then_inc(mv_done, 1)

            def normalise(dst_, src, mv, rs, done):
                for t in range(2):
                    last = v.tensor_scalar(dst_(t), src(t), mv[:, t, 0:1], rs(t), ALU.subtract, ALU.mult)
                last.then_inc(done, 1)

            def prep_stats(par, n):
                dve.wait_ge(S["x_loaded"], 16 * n)
                stats(lambda t: xin[:, par, t, :], st1, mv1, S["st1_done"], S["mv1_done"], n)

            def prep_norm(par, n, reuse):
                dve.wait_ge(S["rs1_done"], n)
                if reuse is not None:
                    dve.wait_ge(S["xn_tr"], reuse)
                normalise(lambda t: xn[:, t, :], lambda t: xin[:, par, t, :], mv1,
                          lambda t: rs1[:, t:t + 1], S["xn_ready"])

            def prep_split(par, n):
                dve.wait_ge(S["xn_ready"], n)
                v.tensor_copy(xk_hi[:, par], xn[:]).then_inc(S["xk_hi_done"], 1)
                dve.wait_ge(S["xk_hi_done"], n)
                v.tensor_tensor(xk_lo[:, par], xn[:], xk_hi[:, par].bitcast(F32), ALU.subtract)

            def prep_turned(par, n):
                dve.wait_ge(S["xt_hi_done"], n)
                v.tensor_tensor(xt_lo[:, par, :], psM[:, 0:T], xt_hi[:, par, :].bitcast(F32),
                                ALU.subtract).then_inc(S["x_split"], 1)

            dve.memset(pay[:], 0.0)
            prep_stats(0, 1)
            prep_norm(0, 1, None)
            prep_split(0, 1)
            for j in range(HD // P):
                dve.wait_ge(S["ab_hi_done"], j + 1)
                v.tensor_tensor(ab_lo[:, 2 * j:2 * j + 2].rearrange("p h m c -> p h (m c)"), psP[:, :, 0:2 * P],
                                ab_hi[:, 2 * j:2 * j + 2].rearrange("p h m c -> p h (m c)").bitcast(F32),
                                ALU.subtract).then_inc(S["ab_split"], 1)
            prep_turned(0, 1)
            dve.wait_ge(S["bias_done"], 1)
            b1v = w1g[:, :, FB * P:FB * P + FB]
            v.tensor_tensor(b1v, psU[:, 0:E * FB].rearrange("p (e j) -> p e j", e=E), b1v,
                            ALU.add).then_inc(S["bias_copied"], 1)
            for e in range(E):
                v.tensor_scalar(w1g[:, e, 0:FB * P], w1g[:, e, 0:FB * P], gam[:, e:e + 1], None, ALU.mult)

            def slot(g0, b0, s, live, live_b):
                r, db = s % PAIRS, s // PAIRS
                if live(2):
                    p2 = (s - 2) % 4
                    dve.wait_ge(S["probs_ready"], 2 * (g0 + s - 1))
                    v.reciprocal(rinv[:, p2].rearrange("p h q -> p (h q)"),
                                 rsum[:, p2].rearrange("p h q -> p (h q)")).then_inc(S["rinv_ready"], 1)
                if live(0):
                    dve.wait_ge(S["t_hi_done"], g0 + s + 1)
                    v.tensor_tensor(t_lo[:, s % 2], psT[:], t_hi[:, s % 2].bitcast(F32),
                                    ALU.subtract).then_inc(S["t_split"], 1)

                def score_max(h):
                    p1 = (s - 1) % 4
                    dve.wait_ge(S["s_ready"], 2 * (g0 + s - 1) + 1 + h)
                    for q, (a, z) in enumerate(((0, P), (P, 384))):
                        last = v.tensor_reduce(nmax[:, p1, h, q:q + 1], psS[:, h, a:z], AX.X, ALU.max, negate=True)
                    last.then_inc(S["nmax_ready"], 1)

                if live(1):
                    score_max(0)
                misc(g0, b0, s, live, live_b)
                if live(3):
                    dve.wait_ge(S["p_hi_done"], g0 + s - 2)
                    v.tensor_tensor(p_lo[:, (s - 3) % 2], psP[:, :, 0:384], p_hi[:, (s - 3) % 2].bitcast(F32),
                                    ALU.subtract).then_inc(S["p_split"], 1)
                if live(1):
                    score_max(1)
                if live(4):
                    dve.wait_ge(S["z_hi_done"], g0 + s - 3)
                    v.tensor_tensor(z_lo[:, (s - 4) % 2], psZ[:], z_hi[:, (s - 4) % 2].bitcast(F32),
                                    ALU.subtract).then_inc(S["z_split"], 1)

            def misc(g0, b0, s, live, live_b):
                r, db = s % PAIRS, s // PAIRS
                if r == 0 and live_b(2):
                    n = b0 + db - 1
                    dve.wait_ge(S["rs2_done"], n)
                    normalise(lambda t: an[:, t, :], lambda t: psM[:, t * P:(t + 1) * P], mv2,
                              lambda t: rs2[:, t:t + 1], S["a_norm"])
                if r == 1 and live_b(2):
                    n = b0 + db - 1
                    dve.wait_ge(S["x1_ready"], n)
                    stats(lambda t: pay[:, db, t, 0:P], st3, mv3, S["st3_done"], S["mv3_done"], n)
                if r == 2 and live_b(2):
                    n = b0 + db - 1
                    dve.wait_ge(S["r3_steps"], 6 * n)
                    normalise(lambda t: fn[:, t, :], lambda t: pay[:, db, t, 0:P], mv3,
                              lambda t: pay[:, db, t, C_RSTD:C_RSTD + 1], S["f_ready"])
                    v.scalar_tensor_tensor(pay[:, db, :, C_SHIFT], mv3[:, :, 0], -1.0, pay[:, db, :, C_RSTD],
                                           ALU.mult, ALU.mult)
                    v.tensor_copy(pay[:, db, :, C_ID].bitcast(U32), idf[:, db, :])
                    v.tensor_scalar(idf[:, 1 - db, :], idf[:, db, :], float(T), None, ALU.add)
                if r == 2 and live_b(-1):
                    prep_stats((db + 1) % 2, b0 + db + 2)
                if r == 3 and live_b(-1):
                    prep_norm((db + 1) % 2, b0 + db + 2, b0 + db + 1)
                if r == 4 and live_b(-1):
                    if live_b(1):
                        dve.wait_ge(S["z_ready"], PAIRS * (b0 + db))
                    prep_split((db + 1) % 2, b0 + db + 2)
                if r == 4 and live_b(2):
                    n = b0 + db - 2
                    dve.wait_ge(S["scored"], n + 1)
                    scv = psM[:, 0:2 * E].rearrange("p (t e) -> p t e", t=2)
                    over = lambda a: a.unsqueeze(2).broadcast_to([P, 2, E])
                    rank_e = rev_e[:].unsqueeze(1).broadcast_to([P, 2, E])
                    best = pay[:, db, :, C_SCORE]

                    def link(ins, k):
                        ins.then_inc(S["argmax_steps"], 1)
                        dve.wait_ge(S["argmax_steps"], 4 * n + k)

                    link(v.tensor_reduce(best, scv, AX.X, ALU.max), 1)
                    link(v.tensor_tensor(hits[:], scv, over(best), ALU.is_ge), 2)
                    link(v.tensor_tensor(hitr[:], hits[:], rank_e, ALU.mult), 3)
                    link(v.tensor_reduce(first[:], hitr[:], AX.X, ALU.max), 4)
                    v.tensor_tensor(oh[:], rank_e, over(first[:]), ALU.is_equal).then_inc(S["onehot_ready"], 1)
                if r == 5 and live_b(2):
                    n = b0 + db - 2
                    dve.wait_ge(S["ranked"], n + 1)
                    v.tensor_tensor(dsum[:], psM[:, 0:2 * E].rearrange("p (t e) -> p t e", t=2),
                                    base[:, db, :].unsqueeze(1).broadcast_to([P, 2, E]), ALU.add)
                    v.tensor_tensor(base[:, 1 - db, :], psM[:, 2 * E:3 * E], base[:, db, :],
                                    ALU.add).then_inc(S["dest_steps"], 1)
                    dve.wait_ge(S["dest_steps"], 3 * n + 1)
                    v.tensor_tensor(dsel[:], dsum[:], oh[:], ALU.mult).then_inc(S["dest_steps"], 1)
                    dve.wait_ge(S["dest_steps"], 3 * n + 2)
                    v.tensor_reduce(dstf[:], dsel[:], AX.X, ALU.add).then_inc(S["dest_steps"], 1)
                    dve.wait_ge(S["dest_steps"], 3 * n + 3)
                    v.tensor_copy(dst[:, db, :], dstf[:]).then_inc(S["dest_ready"], 1)
                if r == 6 and live_b(-1):
                    prep_turned((db + 1) % 2, b0 + db + 2)
                if r == 7 and live_b(1):
                    n = b0 + db
                    dve.wait_ge(S["a_tr"], n)
                    stats(lambda t: psM[:, t * P:(t + 1) * P], st2, mv2, S["st2_done"], S["mv2_done"], n)

            dve.wait_ge(S["consts_ready"], 1)
            phases(dve, slot)
            FFN["dve"](dve)

        @block.gpsimd
        def _(pool):
            g = nc.gpsimd

            def inv_sqrt(dst_, ve, src, mv_done, ve_done, done, n):
                pool.wait_ge(mv_done, n)
                g.tensor_tensor(ve[:], src, eps_t[:], ALU.add).then_inc(ve_done, 1)
                pool.wait_ge(ve_done, n)
                g.tensor_tensor(dst_, ve[:], neg_half[:], ALU.pow).then_inc(done, 1)

            steps = ctx.enter_context(nc.semaphore("const_steps"))
            nst = [0]

            def step(ins):
                nst[0] += 1
                ins.then_inc(steps, 1)
                pool.wait_ge(steps, nst[0])

            step(g.memset(neg_half[:], -0.5))
            step(g.memset(eps_t[:], EPS))
            inv_sqrt(rs1[:], ve1, mv1[:, :, 1], S["mv1_done"], S["ve1_done"], S["rs1_done"], 1)
            step(g.memset(ident[:], 0.0))
            step(g.affine_select(ident[:], ident[:], [[-1, P]], ALU.not_equal, 1.0, base=0, channel_multiplier=1))
            step(g.tensor_copy(identb[:], ident[:]))
            step(g.memset(onesb[:], 1.0))
            step(g.memset(maskb[:], 0.0))
            step(g.affine_select(maskb[:], maskb[:], [[-1, P]], ALU.is_ge, MASKED, base=0, channel_multiplier=1))
            step(g.affine_select(before[:], onesb[:], [[1, P]], ALU.is_gt, 0.0, base=0, channel_multiplier=-1))
            step(g.iota(iota_i[:], [[-1, E]], base=E, channel_multiplier=0))
            step(g.tensor_copy(rev_e[:], iota_i[:]))
            step(g.iota(iota_i[:], [[REGION, E]], base=0, channel_multiplier=0))
            step(g.tensor_copy(base[:, 0, :], iota_i[:]))
            step(g.tensor_copy(regb[:], iota_i[:]))
            step(g.iota(iota_i[:, 0:1], [[0, 1]], base=0, channel_multiplier=1))
            step(g.tensor_copy(pidx[:], iota_i[:, 0:1]))
            step(g.iota(tixi[:], [[1, TILES]], base=0, channel_multiplier=0))
            step(g.tensor_copy(tix[:], tixi[:]))
            step(g.memset(padr[:], 0.0))
            g.memset(padr[:, C_ID:C_ID + 1].bitcast(U32), NOWHERE).then_inc(S["pads_ready"], 1)
            step(g.iota(iota_i[:, 0:2], [[P, 2]], base=0, channel_multiplier=1))
            g.tensor_copy(idf[:, 0, :], iota_i[:, 0:2]).then_inc(S["consts_ready"], 1)

            def slot(g0, b0, s, live, live_b):
                r, db = s % PAIRS, s // PAIRS
                if live(2):
                    p2 = (s - 2) % 4
                    pool.wait_ge(S["rinv_ready"], g0 + s - 1)
                    for q, (a, z) in enumerate(((0, P), (P, 384))):
                        pr = prob[:, p2, :, a:z]
                        last = g.tensor_tensor(pr, pr, rinv[:, p2, :, q:q + 1].broadcast_to([P, 2, z - a]), ALU.mult)
                    last.then_inc(S["norm_ready"], 1)
                if r == 0 and live_b(2):
                    n = b0 + db - 1
                    pool.wait_ge(S["a_norm"], n)
                    pool.wait_ge(S["xr_loaded"], 16 * n)
                    g.tensor_tensor(pay[:, db, :, 0:P], an[:], xres[:, db], ALU.add).then_inc(S["x1_ready"], 1)
                if r == 1 and live_b(2):
                    n = b0 + db - 2
                    k = [6 * n]

                    def link(ins):
                        k[0] = k[0] + 1
                        ins.then_inc(S["r3_steps"], 1)
                        pool.wait_ge(S["r3_steps"], k[0])

                    rs3 = pay[:, db, :, C_RSTD]
                    pool.wait_ge(S["mv3_done"], n + 1)
                    link(g.tensor_tensor(ve3[:], mv3[:, :, 1], eps_t[:], ALU.add))
                    link(g.tensor_tensor(rs3, ve3[:], neg_half[:], ALU.pow))
                    link(g.tensor_tensor(w3[:, 0, :], mv3[:, :, 1], rs3, ALU.mult))
                    link(g.tensor_tensor(w3[:, 1, :], w3[:, 0, :], rs3, ALU.mult))
                    link(g.tensor_tensor(w3[:, 2, :], w3[:, 1, :], eps_t[:], ALU.add))
                    g.tensor_tensor(pay[:, db, :, C_RSTD2], w3[:, 2, :], neg_half[:],
                                    ALU.pow).then_inc(S["r3_steps"], 1)
                if r == 2 and live_b(-1):
                    inv_sqrt(rs1[:], ve1, mv1[:, :, 1], S["mv1_done"], S["ve1_done"], S["rs1_done"], b0 + db + 2)
                if r == 5 and live_b(2):
                    wait_apart(pool, S["dest_ready"], b0 + db - 1)
                    for t in range(2):
                        g.indirect_dma_start(rows, bass.IndirectOffsetOnAxis(ap=dst[:, db, t:t + 1], axis=0),
                                             pay[:, db, t, :], None).then_inc(S["scattered"], 16)
                if r == 7 and live_b(2):
                    pool.wait_ge(S["scattered"], 32 * (b0 + db - 1))
                if r == 7 and live_b(1):
                    inv_sqrt(rs2[:], ve2, mv2[:, :, 1], S["mv2_done"], S["ve2_done"], S["rs2_done"], b0 + db)

            phases(pool, slot)
            FFN["pool"](pool)


def kernel(L0_attn_x, L0_attn_w_kv_down, L0_attn_w_kv_up, L0_attn_w_q, L0_attn_w_out, L0_ffn_centroids,
           L0_ffn_gamma, L0_ffn_beta, L0_ffn_W1, L0_ffn_b1, L0_ffn_W2, L0_ffn_b2):
    import numpy as np
    import concourse.bacc as bacc
    from concourse.bass_utils import run_bass_kernel_spmd

    shape = L0_attn_x.shape
    C = shape[-1]
    HD = L0_attn_w_q.shape[1]
    E, F, _ = L0_ffn_W1.shape
    lay = lambda a, *perm: np.ascontiguousarray(np.transpose(a, perm))
    arrays = {
        "x": np.asarray(L0_attn_x).reshape(-1, C),
        "wd_t": lay(L0_attn_w_kv_down, 1, 0),
        "wup": np.asarray(L0_attn_w_kv_up),
        "wq_t": lay(np.asarray(L0_attn_w_q).reshape(C, HD // P, P), 2, 1, 0),
        "wo": lay(np.asarray(L0_attn_w_out).reshape(HD // P, P, C), 1, 0, 2),
        "cent_t": lay(L0_ffn_centroids, 1, 0),
        "gamma_t": lay(L0_ffn_gamma, 1, 0),
        "beta_t": lay(L0_ffn_beta, 1, 0),
        "w1_t": lay(L0_ffn_W1, 2, 0, 1),
        "b1": lay(np.asarray(L0_ffn_b1).reshape(E, F // P, P), 2, 0, 1),
        "w2_t": lay(np.asarray(L0_ffn_W2).reshape(E, C, F // P, P), 3, 0, 2, 1),
        "b2": np.asarray(L0_ffn_b2),
    }
    arrays = {k: np.ascontiguousarray(a) for k, a in arrays.items()}
    nc = bacc.Bacc("TRN2", target_bir_lowering=False, num_devices=1)
    args = [nc.dram_tensor(k, a.shape, mybir.dt.from_np(a.dtype), kind="ExternalInput").ap()
            for k, a in arrays.items()]
    out = nc.dram_tensor("out", arrays["x"].shape, F32, kind="ExternalOutput").ap()
    block_kernel(nc, *args, out)
    r = run_bass_kernel_spmd(nc, [arrays], core_ids=[0])
    return r.results[0]["out"].reshape(shape)
```

```python
from contextlib import ExitStack

import concourse.bass as bass
from concourse import mybir

ALU = mybir.AluOpType
ACT = mybir.ActivationFunctionType
AX = mybir.AxisListType
F32 = mybir.dt.float32
F32R = mybir.dt.float32r
BF16 = mybir.dt.bfloat16
U32 = mybir.dt.uint32
I32 = mybir.dt.int32

P = 128
EPS = 1e-5
MASKED = -3.0e38

C_RSTD = 128
C_SHIFT = 129
C_RSTD2 = 130
C_SCORE = 131
C_ID = 132
ROW = 136
NOWHERE = 1 << 20


def block_kernel(nc, x, wd_t, wup, wq_t, wo, cent_t, gamma_t, beta_t, ffn_w, out):
    ntok, C = x.shape
    T = 256
    NB = ntok // T
    HD = wup.shape[1] // 2
    D = 64
    NH = HD // D
    E = cent_t.shape[1]
    FB = ffn_w.shape[2] // (2 * P)
    PAIRS = NH // 2
    SLOTS = 2 * PAIRS
    ITERS = NB // 2
    REGION = ntok + T
    TILES = ntok // T + E - 1
    TILES += -TILES % 8
    assert C == P and PAIRS == 8 and NB % 2 == 0 and ITERS >= 2

    rows = nc.dram_tensor("routed_rows", [E * REGION + T, ROW], F32, kind="Internal").ap()

    with ExitStack() as ctx:
        def sb(name, shape, dt=F32):
            return ctx.enter_context(nc.sbuf_tensor(name, shape, dt))

        def ps(name, shape, dt=F32):
            return ctx.enter_context(nc.psum_tensor(name, shape, dt))

        def sem(name):
            return ctx.enter_context(nc.semaphore(name))

        psT = ps("psT", [P, 2, T])
        psS = ps("psS", [P, 2, 512])
        psP = ps("psP", [P, 2, 512])
        psZ = ps("psZ", [P, 2, T])
        psU = ps("psU", [P, 512])
        psM = ps("psM", [P, 512])

        ab_hi = sb("ab_hi", [P, NH, 2, P], F32R)
        ab_lo = sb("ab_lo", [P, NH, 2, P], F32R)
        cent = sb("cent", [P, E])
        gam = sb("gam", [P, E])
        bet = sb("bet", [P, E])
        wx = sb("wx", [P, E, 2 * FB * P + FB + 1])
        B1, W2 = FB * P, FB * P + FB

        ident = sb("ident", [P, P])
        identb = sb("identb", [P, P], BF16)
        maskb = sb("maskb", [P, P], BF16)
        before = sb("before", [P, P], BF16)
        onesb = sb("onesb", [P, P], BF16)
        neg_half = sb("neg_half", [P, 2])
        eps_t = sb("eps_t", [P, 2])
        rev_e = sb("rev_e", [P, E])
        iota_i = sb("iota_i", [P, E], I32)

        xin = sb("xin", [P, 2, 2, P])
        xres = sb("xres", [P, 2, 2, P])
        st1 = sb("st1", [P, 2, 6])
        mv1 = sb("mv1", [P, 2, 2])
        ve1 = sb("ve1", [P, 2])
        rs1 = sb("rs1", [P, 2])
        xn = sb("xn", [P, 2, P])
        xk_hi = sb("xk_hi", [P, 2, 2, P], F32R)
        xk_lo = sb("xk_lo", [P, 2, 2, P], F32R)
        xt_hi = sb("xt_hi", [P, 2, T], F32R)
        xt_lo = sb("xt_lo", [P, 2, T], F32R)
        t_hi = sb("t_hi", [P, 2, 2, T], F32R)
        t_lo = sb("t_lo", [P, 2, 2, T], F32R)
        nmax = sb("nmax", [P, 4, 2, 2])
        rsum = sb("rsum", [P, 4, 2, 2])
        rinv = sb("rinv", [P, 4, 2, 2])
        prob = sb("prob", [P, 4, 2, 384])
        p_hi = sb("p_hi", [P, 2, 2, 384], F32R)
        p_lo = sb("p_lo", [P, 2, 2, 384], F32R)
        z_hi = sb("z_hi", [P, 2, 2, T], F32R)
        z_lo = sb("z_lo", [P, 2, 2, T], F32R)
        at = sb("at", [P, T])
        st2 = sb("st2", [P, 2, 6])
        mv2 = sb("mv2", [P, 2, 2])
        ve2 = sb("ve2", [P, 2])
        rs2 = sb("rs2", [P, 2])
        an = sb("an", [P, 2, P])
        pay = sb("pay", [P, 2, 2, ROW])
        st3 = sb("st3", [P, 2, 6])
        mv3 = sb("mv3", [P, 2, 2])
        ve3 = sb("ve3", [P, 2])
        w3 = sb("w3", [P, 3, 2])
        fn = sb("fn", [P, 2, P])
        ft = sb("ft", [P, T])
        hits = sb("hits", [P, 2, E])
        hitr = sb("hitr", [P, 2, E])
        first = sb("first", [P, 2])
        oh = sb("oh", [P, 2, E], BF16)
        base = sb("base", [P, 2, E])
        dsum = sb("dsum", [P, 2, E])
        dsel = sb("dsel", [P, 2, E])
        dstf = sb("dstf", [P, 2])
        dst = sb("dst", [P, 2, 2], U32)
        idf = sb("idf", [P, 2, 2])

        wd_s = sb("wd_s", [P, P])
        wup_s = sb("wup_s", [P, 2 * HD])
        wq_s = sb("wq_s", [P, HD // P, P])
        wo_s = sb("wo_s", [P, HD // P, P])
        kv_t = sb("kv_t", [P, 2, HD // P, P])

        names = """w_loaded ffnw_loaded consts_ready kv_done kv_copied ab_done ab_hi_done ab_split bias_done bias_copied
            x_loaded xr_loaded st1_done mv1_done ve1_done rs1_done xn_ready xk_hi_done xn_tr xt_hi_done x_split
            t_ready t_hi_done t_split s_ready nmax_ready probs_ready rinv_ready norm_ready pt_ready p_hi_done p_split
            z_ready z_hi_done z_split u_done u_copied a_tr st2_done mv2_done ve2_done rs2_done a_norm x1_ready
            st3_done mv3_done r3_steps f_ready f_tr ft_ready scored argmax_steps onehot_ready ranked dest_steps
            dest_ready scattered"""
        S = {n: sem(n) for n in names.split()}
        FU = 8
        W1W = FB * P + FB
        WW = W1W + FB * P + 1
        regb = sb("regb", [P, E])
        padr = sb("padr", [P, 2, ROW])
        cnt = sb("cnt", [P, E])
        cnti = sb("cnti", [P, 2, E], I32)
        ends = sb("ends", [P, E], I32)
        ntile = sb("ntile", [P, E])
        csum = sb("csum", [P, 3, E])
        tix = sb("tix", [P, TILES])
        tixi = sb("tixi", [P, TILES], I32)
        past = sb("past", [P, TILES, E])
        pastn = sb("pastn", [P, TILES, E])
        texp = sb("texp", [P, TILES])
        tpre = sb("tpre", [P, TILES])
        trow = sb("trow", [P, 3, TILES])
        table = sb("table", [P, TILES, 2], I32)
        fin = sb("fin", [P, FU, 2, ROW])
        ff = sb("ff", [P, FU, 2, P])
        nn = sb("nn", [P, 2, P])
        nt = sb("nt", [P, 2, T])
        wst = sb("wst", [P, 4, WW])
        hid = sb("hid", [P, 2, FB, T])
        yt = sb("yt", [P, T])
        ea = sb("ea", [P, FU, 2])
        ea1 = sb("ea1", [P, 2])
        alpha = sb("alpha", [P, FU, 2])
        gg = sb("gg", [P, 2, 2, P])
        gst = sb("gst", [P, 2, 6])
        carry = sb("carry", [P, 1])
        gmv = sb("gmv", [P, 2, 2, 2])
        gve = sb("gve", [P, 2])
        grs = sb("grs", [P, 2, 2])
        on = sb("on", [P, 2, P])
        res = sb("res", [P, 2, 2, P])
        for n in """pads_ready pad_stored spare_stored ends_ready table_steps table_ready wst_ready exp_done nt_ready
            relu_a relu_d ff_done nn_ready n_tr h_done yt_done yt_ready y_tr alpha_steps g_steps gmv_ready gve_done
            grs_ready on_ready res_ready""".split():
            S[n] = sem(n)
        f_loaded = [sem(f"f_loaded{i}") for i in range(FU)]
        stored = [sem(f"stored{i}") for i in range(FU)]
        psH = psS[:].rearrange("p b (j t) -> p (b j) t", j=2)
        psN, psY, psO = psU, psT, psZ

        def ffn_phases(eng, slot):
            for s in range(FU):
                slot(0, 0, s, lambda lag: s >= lag)
            with eng.Fori(1, TILES // FU) as it:
                m0 = eng.snap(it * FU)
                n0 = eng.snap(it * 16)
                for s in range(FU):
                    slot(m0, n0, s, lambda lag: True)
            for s in range(5):
                slot(TILES, TILES // FU * 16, s, lambda lag: s < lag)

        def ffn_sp(sp):
            sp.wait_ge(S["ends_ready"], 1)
            for e in range(E):
                row = sp.value_load(ends[0:1, e:e + 1], min_val=0, max_val=(e + 1) * REGION - T)
                sp.dma_start(rows[bass.ds(row, T), :].rearrange("(t p) c -> p t c", p=P),
                             padr[:]).then_inc(S["pad_stored"], 16)
            sp.wait_ge(S["table_ready"], 1)
            sp.wait_ge(S["scattered"], 32 * NB)
            sp.wait_ge(S["pad_stored"], 16 * E)
            sp.wait_ge(S["spare_stored"], 16)

            def slot(m0, n0, s, live):
                if not live(0):
                    return
                if live(FU):
                    sp.wait_ge(stored[s], n0 + n0)
                row = sp.value_load(table[0:1, bass.ds(m0 + s, 1), 0], min_val=0, max_val=E * REGION)
                sp.dma_start(fin[:, s], rows[bass.ds(row, T), :].rearrange("(t p) c -> p t c", p=P)
                             ).then_inc(f_loaded[s], 16)

            ffn_phases(sp, slot)

        def ffn_pe(pe):
            mm = nc.tensor.matmul

            def slot(m0, n0, s, live):
                if live(3):
                    pe.wait_ge(S["yt_ready"], m0 + s - 2)
                    if live(4):
                        pe.wait_ge(S["g_steps"], 2 * (m0 + s - 3))
                    for t in range(2):
                        last = nc.tensor.transpose(psO[:, t, 0:P], yt[:, t * P:(t + 1) * P], ident[:])
                    last.then_inc(S["y_tr"], 1)
                if live(1):
                    pe.wait_ge(S["nt_ready"], m0 + s)
                    pe.wait_ge(S["wst_ready"], m0 + s)
                    if live(2):
                        pe.wait_ge(S["relu_a"], m0 + s - 1)
                        pe.wait_ge(S["relu_d"], m0 + s - 1)
                    for j in range(FB):
                        last = mm(psH[:, j, :], wst[:, (s - 1) % 4, j * P:(j + 1) * P], nt[:, (s - 1) % 2, :],
                                  start=True, stop=True)
                    last.then_inc(S["h_done"], 1)
                if live(0):
                    pe.wait_ge(S["nn_ready"], m0 + s + 1)
                    if live(1):
                        pe.wait_ge(S["nt_ready"], m0 + s)
                    for t in range(2):
                        last = nc.tensor.transpose(psN[:, t * P:(t + 1) * P], nn[:, t, :], ident[:])
                    last.then_inc(S["n_tr"], 1)
                if live(2):
                    pe.wait_ge(S["relu_a"], m0 + s - 1)
                    pe.wait_ge(S["relu_d"], m0 + s - 1)
                    if live(3):
                        pe.wait_ge(S["yt_ready"], m0 + s - 2)
                    for j in range(FB):
                        a = W1W + j * P
                        last = mm(psY[:, 0, :], wst[:, (s - 2) % 4, a:a + P], hid[:, s % 2, j, :],
                                  start=(j == 0), stop=(j == FB - 1))
                    last.then_inc(S["yt_done"], 1)

            ffn_phases(pe, slot)

        def ffn_act(act):
            act.wait_ge(S["table_ready"], 1)

            def slot(m0, n0, s, live):
                if live(0):
                    if live(4):
                        act.wait_ge(S["yt_done"], m0 + s - 3)
                        act.wait_ge(S["yt_ready"], m0 + s - 3)
                        act.wait_ge(S["relu_d"], m0 + s - 3)
                    e = act.value_load(table[0:1, bass.ds(m0 + s, 1), 1], min_val=0, max_val=E - 1)
                    nc.scalar.activation(wst[:, s % 4, :], wx[:, bass.ds(e, 1), :].rearrange("p a c -> p (a c)"),
                                         ACT.Copy).then_inc(S["wst_ready"], 1)
                    act.wait_ge(f_loaded[s], n0 + 16)
                    nc.scalar.activation(ea[:, s, :], fin[:, s, :, C_SCORE], ACT.Exp,
                                         scale=-1.0).then_inc(S["exp_done"], 1)
                    act.wait_ge(S["n_tr"], m0 + s + 1)
                    if live(2):
                        act.wait_ge(S["h_done"], m0 + s - 1)
                    nc.scalar.activation(nt[:, s % 2, :], psN[:, 0:T], ACT.Copy).then_inc(S["nt_ready"], 1)
                if live(1):
                    act.wait_ge(S["h_done"], m0 + s)
                    if live(3):
                        act.wait_ge(S["yt_done"], m0 + s - 2)
                    w = wst[:, (s - 1) % 4, :]
                    for j in range(2):
                        last = nc.scalar.activation(hid[:, (s - 1) % 2, j, :], psH[:, j, :], ACT.Relu,
                                                    bias=w[:, FB * P + j:FB * P + j + 1])
                    last.then_inc(S["relu_a"], 1)
                if live(2):
                    act.wait_ge(S["yt_done"], m0 + s - 1)
                    if live(3):
                        act.wait_ge(S["y_tr"], m0 + s - 2)
                    nc.scalar.activation(yt[:], psY[:, 0, :], ACT.Identity,
                                         bias=wst[:, (s - 2) % 4, WW - 1:WW]).then_inc(S["yt_ready"], 1)

            ffn_phases(act, slot)

        def ffn_dve(dve):
            v = nc.vector
            k = [0]

            def link(ins):
                k[0] += 1
                ins.then_inc(S["table_steps"], 1)
                dve.wait_ge(S["table_steps"], k[0])

            dve.wait_ge(S["dest_ready"], NB)
            last_base = base[:, NB % 2, :]
            v.tensor_copy(ends[:], last_base).then_inc(S["ends_ready"], 1)
            link(v.tensor_tensor(cnt[:], last_base, regb[:], ALU.subtract))
            link(v.tensor_scalar(cnti[:, 0, :], cnt[:], float(T - 1), None, ALU.add))
            link(v.tensor_single_scalar(cnti[:, 1, :], cnti[:, 0, :], 8, ALU.arith_shift_right))
            link(v.tensor_copy(ntile[:], cnti[:, 1, :]))
            src = ntile[:]
            for n, d in enumerate((1, 2, 4)):
                v.tensor_copy(csum[:, n, 0:d], src[:, 0:d])
                link(v.tensor_tensor(csum[:, n, d:E], src[:, d:E], src[:, 0:E - d], ALU.add))
                src = csum[:, n, :]
            link(v.tensor_tensor(past[:], tix[:].unsqueeze(2).broadcast_to([P, TILES, E]),
                                 src.unsqueeze(1).broadcast_to([P, TILES, E]), ALU.is_ge))
            v.tensor_reduce(texp[:], past[:], AX.X, ALU.add)
            link(v.tensor_tensor(pastn[:], past[:], ntile[:].unsqueeze(1).broadcast_to([P, TILES, E]), ALU.mult))
            link(v.tensor_reduce(tpre[:], pastn[:], AX.X, ALU.add))
            link(v.tensor_tensor(trow[:, 0, :], tix[:], tpre[:], ALU.subtract))
            link(v.tensor_scalar(trow[:, 1, :], trow[:, 0, :], float(T), None, ALU.mult))
            link(v.scalar_tensor_tensor(trow[:, 2, :], texp[:], float(REGION), trow[:, 1, :], ALU.mult, ALU.add))
            v.tensor_scalar(table[:, :, 0], trow[:, 2, :], float(E * REGION), None, ALU.min)
            v.tensor_scalar(table[:, :, 1], texp[:], float(E - 1), None, ALU.min).then_inc(S["table_ready"], 1)

            def slot(m0, n0, s, live):
                if live(4):
                    b = s % 2
                    dve.wait_ge(S["grs_ready"], m0 + s - 3)
                    if live(5):
                        dve.wait_ge(S["res_ready"], m0 + s - 4)
                    for t in range(2):
                        last = v.tensor_scalar(on[:, t, :], gg[:, b, t, :], gmv[:, b, t, 0:1], grs[:, b, t:t + 1],
                                               ALU.subtract, ALU.mult)
                    last.then_inc(S["on_ready"], 1)
                if live(0):
                    dve.wait_ge(f_loaded[s], n0 + 16)
                    for t in range(2):
                        last = v.tensor_scalar(ff[:, s, t, :], fin[:, s, t, 0:P], fin[:, s, t, C_RSTD:C_RSTD + 1],
                                               fin[:, s, t, C_SHIFT:C_SHIFT + 1], ALU.mult, ALU.add)
                    last.then_inc(S["ff_done"], 1)
                if live(3):
                    b, sf = (s - 3) % 2, (s - 3) % FU
                    m = m0 + s - 3
                    dve.wait_ge(S["y_tr"], m + 1)
                    for t in range(2):
                        last = v.scalar_tensor_tensor(gg[:, b, t, :], psO[:, t, 0:P], alpha[:, sf, t:t + 1],
                                                      ff[:, sf, t, :], ALU.mult, ALU.add)
                    last.then_inc(S["g_steps"], 1)
                if live(0):
                    dve.wait_ge(S["ff_done"], m0 + s + 1)
                    if live(1):
                        dve.wait_ge(S["n_tr"], m0 + s)
                    for t in range(2):
                        last = v.tensor_scalar(nn[:, t, :], ff[:, s, t, :], fin[:, s, t, C_RSTD2:C_RSTD2 + 1], None,
                                               ALU.mult)
                    last.then_inc(S["nn_ready"], 1)
                if live(3):
                    dve.wait_ge(S["g_steps"], 2 * m + 1)
                    for t in range(2):
                        last = v.bn_stats(gst[:, t, :], gg[:, b, t, :])
                    last.then_inc(S["g_steps"], 1)
                if live(0):
                    dve.wait_ge(S["exp_done"], m0 + s + 1)
                    v.tensor_scalar(ea1[:], ea[:, s, :], 1.0, None, ALU.add).then_inc(S["alpha_steps"], 1)
                if live(3):
                    dve.wait_ge(S["g_steps"], 2 * m + 2)
                    v.tensor_copy(carry[:], gst[:, 0, 0:1])
                    for t in range(2):
                        last = v.bn_aggr(gmv[:, b, t, :], gst[:, t, :])
                    last.then_inc(S["gmv_ready"], 1)
                if live(0):
                    dve.wait_ge(S["alpha_steps"], m0 + s + 1)
                    v.reciprocal(alpha[:, s, :], ea1[:])
                if live(1):
                    dve.wait_ge(S["h_done"], m0 + s)
                    if live(3):
                        dve.wait_ge(S["yt_done"], m0 + s - 2)
                    w = wst[:, (s - 1) % 4, :]
                    for j in range(2, FB):
                        last = v.tensor_scalar(hid[:, (s - 1) % 2, j, :], psH[:, j, :],
                                               w[:, FB * P + j:FB * P + j + 1], 0.0, ALU.add, ALU.max)
                    last.then_inc(S["relu_d"], 1)

            ffn_phases(dve, slot)

        def ffn_pool(pool):
            g = nc.gpsimd

            def slot(m0, n0, s, live):
                if live(4):
                    m, b, sf = m0 + s - 4, (s - 4) % 2, (s - 4) % FU
                    pool.wait_ge(S["on_ready"], m + 1)
                    if live(6):
                        pool.wait_ge(stored[(s - 6) % FU], n0 + n0 + (32 if s >= 6 else 0))
                    g.tensor_tensor(res[:, b], on[:], fin[:, sf, :, 0:P], ALU.add).then_inc(S["res_ready"], 1)
                if live(3):
                    m3, b3 = m0 + s - 3, (s - 3) % 2
                    pool.wait_ge(S["gmv_ready"], m3 + 1)
                    g.tensor_tensor(gve[:], gmv[:, b3, :, 1], eps_t[:], ALU.add).then_inc(S["gve_done"], 1)
                    pool.wait_ge(S["gve_done"], m3 + 1)
                    g.tensor_tensor(grs[:, b3, :], gve[:], neg_half[:], ALU.pow).then_inc(S["grs_ready"], 1)
                if live(4):
                    wait_apart(pool, S["res_ready"], m + 1)
                    for t in range(2):
                        g.indirect_dma_start(out, bass.IndirectOffsetOnAxis(
                            ap=fin[:, sf, t, C_ID:C_ID + 1].bitcast(U32), axis=0), res[:, b, t, :], None,
                            bounds_check=ntok - 1, oob_is_err=False).then_inc(stored[sf], 16)

            ffn_phases(pool, slot)
            for i in range(FU):
                pool.wait_ge(stored[i], TILES // FU * 32)

        FFN = {"sp": ffn_sp, "pe": ffn_pe, "act": ffn_act, "dve": ffn_dve, "pool": ffn_pool}
        block = ctx.enter_context(nc.Block())

        def wait_apart(eng, what, value):
            eng.wait_ge(S["x_loaded"], 16)
            eng.wait_ge(what, value)

        def phases(eng, slot):
            for s in range(SLOTS):
                slot(0, 0, s, lambda lag: s >= lag, lambda d: s // PAIRS >= d)
            if ITERS > 2:
                with eng.Fori(1, ITERS - 1) as it:
                    g0 = eng.snap(it * SLOTS)
                    b0 = eng.snap(it * 2)
                    for s in range(SLOTS):
                        slot(g0, b0, s, lambda lag: True, lambda d: True)
            for s in range(SLOTS):
                slot((ITERS - 1) * SLOTS, NB - 2, s, lambda lag: True,
                     lambda d: s // PAIRS - d < 2)
            for s in range(SLOTS):
                slot(ITERS * SLOTS, NB, s, lambda lag: s < lag, lambda d: s // PAIRS < d)

        @block.sync
        def _(sp):
            for dst_, src in ((wd_s[:], wd_t), (wup_s[:], wup), (wq_s[:], wq_t), (wo_s[:], wo)):
                sp.dma_start(dst_, src).then_inc(S["w_loaded"], 16)

            def load_x(buf, bpar, b, done):
                src = x[bass.ds(b * T, T), :].rearrange("(t p) c -> p t c", p=P)
                sp.dma_start(buf[:, bpar], src).then_inc(done, 16)

            load_x(xin, 0, 0, S["x_loaded"])
            for dst_, src in ((cent[:], cent_t), (gam[:], gamma_t), (bet[:], beta_t),
                              (wx[:, 0:E // 2], ffn_w[:, 0:E // 2]), (wx[:, E // 2:], ffn_w[:, E // 2:])):
                sp.dma_start(dst_, src).then_inc(S["ffnw_loaded"], 16)

            def slot(g0, b0, s, live, live_b):
                r, db = s % PAIRS, s // PAIRS
                if r == 0 and live_b(-1):
                    sp.wait_ge(S["xn_ready"], b0 + db + 1)
                    load_x(xin, (db + 1) % 2, b0 + db + 1, S["x_loaded"])
                if r == 3 and live_b(1):
                    if live_b(2):
                        sp.wait_ge(S["x1_ready"], b0 + db - 1)
                    load_x(xres, (db - 1) % 2, b0 + db - 1, S["xr_loaded"])

            sp.wait_ge(S["pads_ready"], 1)
            sp.dma_start(rows[E * REGION:E * REGION + T, :].rearrange("(t p) c -> p t c", p=P),
                         padr[:]).then_inc(S["spare_stored"], 16)
            phases(sp, slot)
            FFN["sp"](sp)

        @block.tensor
        def _(pe):
            mm = nc.tensor.matmul
            pe.wait_ge(S["w_loaded"], 64)
            for j in range(HD // P):
                if j >= 2:
                    pe.wait_ge(S["kv_copied"], j - 1)
                for kv in range(2):
                    last = mm(psS[:, j % 2, kv * P:(kv + 1) * P],
                              wup_s[:, kv * HD + j * P:kv * HD + (j + 1) * P], wd_s[:], start=True, stop=True)
                last.then_inc(S["kv_done"], 1)
            for j in range(HD // P):
                pe.wait_ge(S["kv_copied"], j + 1)
                ab = (psP, psS)[j % 2]
                if j >= 2:
                    pe.wait_ge(S["ab_split"], j - 1)
                if j == 1:
                    pe.wait_ge(S["kv_copied"], HD // P)
                for e in range(2):
                    h = slice(64 * e, 64 * e + 64)
                    mm(ab[:, e, 0:P], wq_s[h, j, :], kv_t[h, 0, j, :], start=True, stop=True)
                    last = mm(ab[:, e, P:2 * P], kv_t[h, 1, j, :], wo_s[h, j, :], start=True, stop=True)
                last.then_inc(S["ab_done"], 1)
            def turn_x():
                for t in range(2):
                    last = nc.tensor.transpose(psM[:, t * P:(t + 1) * P], xn[:, t, :], ident[:])
                last.then_inc(S["xn_tr"], 1)

            pe.wait_ge(S["consts_ready"], 1)
            pe.wait_ge(S["xn_ready"], 1)
            turn_x()

            def first_bias():
                for e in range(E):
                    for j in range(FB):
                        last = mm(psT[:, 0, e * FB + j:e * FB + j + 1], wx[:, e, j * P:(j + 1) * P], bet[:, e:e + 1],
                                  start=True, stop=True)
                last.then_inc(S["bias_done"], 1)

            def scores(h, tb, xb, freed):
                pe.wait_ge(S["probs_ready"], freed) if freed is not None else None
                diag = psS[:, h, 0:512].rearrange("p (a k) -> p a k", a=2)[:, :, 0:P]
                mm(diag, identb[:], maskb[:].unsqueeze(1).broadcast_to([P, 2, P]),
                   start=True, stop=False, skip_group_check=True)
                for tt, xx in ((t_lo, xt_hi), (t_hi, xt_lo), (t_hi, xt_hi)):
                    last = mm(psS[:, h, 0:P], tt[:, tb, h, 0:P], xx[:, xb, 0:P],
                              start=False, stop=False, skip_group_check=True)
                    last = mm(psS[:, h, P:384], tt[:, tb, h, P:T], xx[:, xb, :],
                              start=False, stop=xx is xt_hi and tt is t_hi, skip_group_check=True)
                last.then_inc(S["s_ready"], 1)

            def slot(g0, b0, s, live, live_b):
                r, db = s % PAIRS, s // PAIRS
                if live(0):
                    if r == 0:
                        pe.wait_ge(S["x_split"], b0 + db + 1)
                    if live(1):
                        pe.wait_ge(S["t_split"], g0 + s)
                    else:
                        pe.wait_ge(S["ab_split"], HD // P)
                    for h in range(2):
                        hh = 2 * r + h
                        mm(psT[:, h, :], ab_lo[:, hh, 0, :], xt_hi[:, db, :], start=True, stop=False)
                        mm(psT[:, h, :], ab_hi[:, hh, 0, :], xt_lo[:, db, :], start=False, stop=False)
                        last = mm(psT[:, h, :], ab_hi[:, hh, 0, :], xt_hi[:, db, :], start=False, stop=True)
                    last.then_inc(S["t_ready"], 1)
                if live(3):
                    p3 = (s - 3) % 4
                    pe.wait_ge(S["norm_ready"], g0 + s - 2)
                    if live(4):
                        pe.wait_ge(S["p_split"], g0 + s - 3)
                    for h in range(2):
                        for k in range(3):
                            last = nc.tensor.transpose(psP[:, h, k * P:(k + 1) * P],
                                                       prob[:, p3, h, k * P:(k + 1) * P], ident[:])
                    last.then_inc(S["pt_ready"], 1)
                if live(1):
                    pe.wait_ge(S["t_split"], g0 + s)
                    xb = ((s - 1) // PAIRS) % 2
                    for h in range(2):
                        scores(h, (s - 1) % 2, xb, 2 * (g0 + s - 2) + 1 + h if live(2) else None)
                if live(4):
                    zb, zx = (s - 4) % 2, ((s - 4) // PAIRS) % 2
                    pe.wait_ge(S["p_split"], g0 + s - 3)
                    if live(5):
                        pe.wait_ge(S["z_split"], g0 + s - 4)
                    terms = ((xk_lo, p_hi), (xk_hi, p_lo), (xk_hi, p_hi))
                    for n, (xx, pp) in enumerate(terms):
                        mm(psZ[:, :, :], xx[:, zx, 0, :], pp[:, zb, :, 0:T], start=(n == 0), stop=False,
                           skip_group_check=True)
                    for n, (xx, pp) in enumerate(terms):
                        last = mm(psZ[:, :, P:T], xx[:, zx, 1, :], pp[:, zb, :, T:384], start=False, stop=(n == 2),
                                  skip_group_check=True)
                    last.then_inc(S["z_ready"], 1)
                if live(5):
                    ub, ur = (s - 5) % 2, (s - 5) % PAIRS
                    pe.wait_ge(S["z_split"], g0 + s - 4)
                    if ur == 0 and live(5 + PAIRS):
                        pe.wait_ge(S["u_copied"], b0 + (s - 5) // PAIRS)
                    for h in range(2):
                        hh = 2 * ur + h
                        for n, (bb, zz) in enumerate(((ab_lo, z_hi), (ab_hi, z_lo), (ab_hi, z_hi))):
                            last = mm(psU[:, 0:T], bb[:, hh, 1, :], zz[:, ub, h, :],
                                      start=(ur == 0 and h == 0 and n == 0),
                                      stop=(ur == PAIRS - 1 and h == 1 and n == 2))
                    last.then_inc(S["u_done"], 1)
                if s == SLOTS - 1 and not live_b(2):
                    pe.wait_ge(S["ffnw_loaded"], 5 * 16)
                if not live(0) and s == 4:
                    first_bias()
                if r == 2 and live_b(2):
                    pe.wait_ge(S["f_ready"], b0 + db - 1)
                    for t in range(2):
                        last = nc.tensor.transpose(psM[:, t * P:(t + 1) * P], fn[:, t, :], ident[:])
                    last.then_inc(S["f_tr"], 1)
                if r == 3 and live_b(2):
                    pe.wait_ge(S["ft_ready"], b0 + db - 1)
                    for t in range(2):
                        last = mm(psM[:, t * E:(t + 1) * E], ft[:, t * P:(t + 1) * P], cent[:], start=True, stop=True)
                    last.then_inc(S["scored"], 1)
                if r == 4 and live_b(2):
                    pe.wait_ge(S["onehot_ready"], b0 + db - 1)
                    mm(psM[:, 0:E], before[:], oh[:, 0, :], start=True, stop=True)
                    mm(psM[:, E:2 * E], before[:], oh[:, 1, :], start=True, stop=False)
                    mm(psM[:, E:2 * E], onesb[:], oh[:, 0, :], start=False, stop=True)
                    mm(psM[:, 2 * E:3 * E], onesb[:], oh[:, 0, :], start=True, stop=False)
                    mm(psM[:, 2 * E:3 * E], onesb[:], oh[:, 1, :], start=False, stop=True).then_inc(S["ranked"], 1)
                if r == 5 and live_b(-1):
                    pe.wait_ge(S["xn_ready"], b0 + db + 2)
                    if live_b(2):
                        pe.wait_ge(S["dest_ready"], b0 + db - 1)
                    turn_x()
                if r == 6 and live_b(1):
                    pe.wait_ge(S["u_copied"], b0 + db)
                    if live_b(-1):
                        pe.wait_ge(S["x_split"], b0 + db + 2)
                    elif live_b(2):
                        pe.wait_ge(S["dest_ready"], b0 + db - 1)
                    for t in range(2):
                        last = nc.tensor.transpose(psM[:, t * P:(t + 1) * P], at[:, t * P:(t + 1) * P], ident[:])
                    last.then_inc(S["a_tr"], 1)

            phases(pe, slot)
            FFN["pe"](pe)

        @block.scalar
        def _(act):
            cp = lambda o, i: nc.scalar.activation(o, i, ACT.Copy)
            for j in range(HD // P):
                act.wait_ge(S["kv_done"], j + 1)
                nc.scalar.activation(kv_t[:, 0, j, :], psS[:, j % 2, 0:P], ACT.Copy, scale=float(D) ** -0.5)
                cp(kv_t[:, 1, j, :], psS[:, j % 2, P:2 * P]).then_inc(S["kv_copied"], 1)
            for j in range(HD // P):
                act.wait_ge(S["ab_done"], j + 1)
                cp(ab_hi[:, 2 * j:2 * j + 2].rearrange("p h m c -> p h (m c)"),
                   (psP, psS)[j % 2][:, :, 0:2 * P]).then_inc(S["ab_hi_done"], 1)

            def xt_top(par):
                cp(xt_hi[:, par, :], psM[:, 0:T]).then_inc(S["xt_hi_done"], 1)

            act.wait_ge(S["xn_tr"], 1)
            xt_top(0)

            def slot(g0, b0, s, live, live_b):
                r, db = s % PAIRS, s // PAIRS
                def exps(h):
                    p1 = (s - 1) % 4
                    act.wait_ge(S["nmax_ready"], 2 * (g0 + s - 1) + 1 + h)
                    for q, (a, z) in enumerate(((0, P), (P, 384))):
                        last = nc.scalar.activation(prob[:, p1, h, a:z], psS[:, h, a:z], ACT.Exp,
                                                    bias=nmax[:, p1, h, q:q + 1],
                                                    accum_out=rsum[:, p1, h, q:q + 1])
                    last.then_inc(S["probs_ready"], 1)

                if r == 3 and live_b(2):
                    act.wait_ge(S["f_tr"], b0 + db - 1)
                    cp(ft[:], psM[:, 0:T]).then_inc(S["ft_ready"], 1)
                if r == 5 and live_b(1):
                    act.wait_ge(S["u_done"], PAIRS * (b0 + db))
                    if live_b(2):
                        act.wait_ge(S["a_tr"], b0 + db - 1)
                    cp(at[:], psU[:, 0:T]).then_inc(S["u_copied"], 1)
                if r == 6 and live_b(-1):
                    act.wait_ge(S["xn_tr"], b0 + db + 2)
                    if live_b(1):
                        act.wait_ge(S["s_ready"], 2 * PAIRS * (b0 + db))
                    xt_top((db + 1) % 2)
                if live(0):
                    act.wait_ge(S["t_ready"], g0 + s + 1)
                    if live(2):
                        act.wait_ge(S["s_ready"], 2 * (g0 + s - 1))
                    cp(t_hi[:, s % 2], psT[:]).then_inc(S["t_hi_done"], 1)
                if live(3):
                    act.wait_ge(S["pt_ready"], g0 + s - 2)
                    if live(5):
                        act.wait_ge(S["z_ready"], g0 + s - 4)
                    cp(p_hi[:, (s - 3) % 2], psP[:, :, 0:384]).then_inc(S["p_hi_done"], 1)
                if live(1):
                    exps(0)
                if live(4):
                    act.wait_ge(S["z_ready"], g0 + s - 3)
                    if live(6):
                        act.wait_ge(S["u_done"], g0 + s - 5)
                    cp(z_hi[:, (s - 4) % 2], psZ[:]).then_inc(S["z_hi_done"], 1)
                if live(1):
                    exps(1)

            phases(act, slot)
            FFN["act"](act)

        @block.vector
        def _(dve):
            v = nc.vector

            def stats(src, st, mv, st_done, mv_done, n):
                for t in range(2):
                    last = v.bn_stats(st[:, t, :], src(t))
                last.then_inc(st_done, 1)
                wait_apart(dve, st_done, n)
                for t in range(2):
                    last = v.bn_aggr(mv[:, t, :], st[:, t, :])
                last.then_inc(mv_done, 1)

            def normalise(dst_, src, mv, rs, done):
                for t in range(2):
                    last = v.tensor_scalar(dst_(t), src(t), mv[:, t, 0:1], rs(t), ALU.subtract, ALU.mult)
                last.then_inc(done, 1)

            def prep_stats(par, n):
                dve.wait_ge(S["x_loaded"], 16 * n)
                stats(lambda t: xin[:, par, t, :], st1, mv1, S["st1_done"], S["mv1_done"], n)

            def prep_norm(par, n, reuse):
                dve.wait_ge(S["rs1_done"], n)
                if reuse is not None:
                    dve.wait_ge(S["xn_tr"], reuse)
                normalise(lambda t: xn[:, t, :], lambda t: xin[:, par, t, :], mv1,
                          lambda t: rs1[:, t:t + 1], S["xn_ready"])

            def prep_split(par, n):
                dve.wait_ge(S["xn_ready"], n)
                v.tensor_copy(xk_hi[:, par], xn[:]).then_inc(S["xk_hi_done"], 1)
                dve.wait_ge(S["xk_hi_done"], n)
                v.tensor_tensor(xk_lo[:, par], xn[:], xk_hi[:, par].bitcast(F32), ALU.subtract)

            def prep_turned(par, n):
                dve.wait_ge(S["xt_hi_done"], n)
                v.tensor_tensor(xt_lo[:, par, :], psM[:, 0:T], xt_hi[:, par, :].bitcast(F32),
                                ALU.subtract).then_inc(S["x_split"], 1)

            def expert_weights():
                dve.wait_ge(S["bias_done"], 1)
                b1v = wx[:, :, B1:W2]
                v.tensor_tensor(b1v, psT[:, 0, 0:E * FB].rearrange("p (e j) -> p e j", e=E), b1v,
                                ALU.add).then_inc(S["bias_copied"], 1)
                for e in range(E):
                    v.tensor_scalar(wx[:, e, 0:FB * P], wx[:, e, 0:FB * P], gam[:, e:e + 1], None, ALU.mult)

            dve.memset(pay[:], 0.0)
            prep_stats(0, 1)
            prep_norm(0, 1, None)
            prep_split(0, 1)
            for j in range(HD // P):
                dve.wait_ge(S["ab_hi_done"], j + 1)
                v.tensor_tensor(ab_lo[:, 2 * j:2 * j + 2].rearrange("p h m c -> p h (m c)"),
                                (psP, psS)[j % 2][:, :, 0:2 * P],
                                ab_hi[:, 2 * j:2 * j + 2].rearrange("p h m c -> p h (m c)").bitcast(F32),
                                ALU.subtract).then_inc(S["ab_split"], 1)
            prep_turned(0, 1)
            def slot(g0, b0, s, live, live_b):
                misc(g0, b0, s, live, live_b)
                if not live(0) and s == 5:
                    expert_weights()
                if live(2):
                    p2 = (s - 2) % 4
                    dve.wait_ge(S["probs_ready"], 2 * (g0 + s - 1))
                    v.reciprocal(rinv[:, p2].rearrange("p h q -> p (h q)"),
                                 rsum[:, p2].rearrange("p h q -> p (h q)")).then_inc(S["rinv_ready"], 1)
                if live(0):
                    dve.wait_ge(S["t_hi_done"], g0 + s + 1)
                    v.tensor_tensor(t_lo[:, s % 2], psT[:], t_hi[:, s % 2].bitcast(F32),
                                    ALU.subtract).then_inc(S["t_split"], 1)

                def score_max(h):
                    p1 = (s - 1) % 4
                    dve.wait_ge(S["s_ready"], 2 * (g0 + s - 1) + 1 + h)
                    for q, (a, z) in enumerate(((0, P), (P, 384))):
                        last = v.tensor_reduce(nmax[:, p1, h, q:q + 1], psS[:, h, a:z], AX.X, ALU.max, negate=True)
                    last.then_inc(S["nmax_ready"], 1)

                if live(1):
                    score_max(0)
                if live(3):
                    dve.wait_ge(S["p_hi_done"], g0 + s - 2)
                    v.tensor_tensor(p_lo[:, (s - 3) % 2], psP[:, :, 0:384], p_hi[:, (s - 3) % 2].bitcast(F32),
                                    ALU.subtract).then_inc(S["p_split"], 1)
                if live(1):
                    score_max(1)
                if live(4):
                    dve.wait_ge(S["z_hi_done"], g0 + s - 3)
                    v.tensor_tensor(z_lo[:, (s - 4) % 2], psZ[:], z_hi[:, (s - 4) % 2].bitcast(F32),
                                    ALU.subtract).then_inc(S["z_split"], 1)

            def misc(g0, b0, s, live, live_b):
                r, db = s % PAIRS, s // PAIRS
                if r == 0 and live_b(2):
                    n = b0 + db - 1
                    dve.wait_ge(S["rs2_done"], n)
                    normalise(lambda t: an[:, t, :], lambda t: psM[:, t * P:(t + 1) * P], mv2,
                              lambda t: rs2[:, t:t + 1], S["a_norm"])
                if r == 1 and live_b(2):
                    n = b0 + db - 1
                    dve.wait_ge(S["x1_ready"], n)
                    stats(lambda t: pay[:, db, t, 0:P], st3, mv3, S["st3_done"], S["mv3_done"], n)
                if r == 2 and live_b(2):
                    n = b0 + db - 1
                    dve.wait_ge(S["r3_steps"], 6 * n - 4)
                    normalise(lambda t: fn[:, t, :], lambda t: pay[:, db, t, 0:P], mv3,
                              lambda t: pay[:, db, t, C_RSTD:C_RSTD + 1], S["f_ready"])
                    v.scalar_tensor_tensor(pay[:, db, :, C_SHIFT], mv3[:, :, 0], -1.0, pay[:, db, :, C_RSTD],
                                           ALU.mult, ALU.mult)
                    v.tensor_copy(pay[:, db, :, C_ID].bitcast(U32), idf[:, db, :])
                    v.tensor_scalar(idf[:, 1 - db, :], idf[:, db, :], float(T), None, ALU.add)
                if r == 2 and live_b(-1):
                    prep_stats((db + 1) % 2, b0 + db + 2)
                if r == 3 and live_b(-1):
                    prep_norm((db + 1) % 2, b0 + db + 2, b0 + db + 1)
                if r == 4 and live_b(-1):
                    if live_b(1):
                        dve.wait_ge(S["z_ready"], PAIRS * (b0 + db))
                    prep_split((db + 1) % 2, b0 + db + 2)
                if r == 4 and live_b(2):
                    n = b0 + db - 2
                    dve.wait_ge(S["scored"], n + 1)
                    scv = psM[:, 0:2 * E].rearrange("p (t e) -> p t e", t=2)
                    over = lambda a: a.unsqueeze(2).broadcast_to([P, 2, E])
                    rank_e = rev_e[:].unsqueeze(1).broadcast_to([P, 2, E])
                    best = pay[:, db, :, C_SCORE]

                    def link(ins, k):
                        ins.then_inc(S["argmax_steps"], 1)
                        dve.wait_ge(S["argmax_steps"], 4 * n + k)

                    link(v.tensor_reduce(best, scv, AX.X, ALU.max), 1)
                    link(v.tensor_tensor(hits[:], scv, over(best), ALU.is_ge), 2)
                    link(v.tensor_tensor(hitr[:], hits[:], rank_e, ALU.mult), 3)
                    link(v.tensor_reduce(first[:], hitr[:], AX.X, ALU.max), 4)
                    v.tensor_tensor(oh[:], rank_e, over(first[:]), ALU.is_equal).then_inc(S["onehot_ready"], 1)
                if r == 5 and live_b(2):
                    n = b0 + db - 2
                    dve.wait_ge(S["ranked"], n + 1)
                    v.tensor_tensor(dsum[:], psM[:, 0:2 * E].rearrange("p (t e) -> p t e", t=2),
                                    base[:, db, :].unsqueeze(1).broadcast_to([P, 2, E]), ALU.add)
                    v.tensor_tensor(base[:, 1 - db, :], psM[:, 2 * E:3 * E], base[:, db, :],
                                    ALU.add).then_inc(S["dest_steps"], 1)
                    dve.wait_ge(S["dest_steps"], 3 * n + 1)
                    v.tensor_tensor(dsel[:], dsum[:], oh[:], ALU.mult).then_inc(S["dest_steps"], 1)
                    dve.wait_ge(S["dest_steps"], 3 * n + 2)
                    v.tensor_reduce(dstf[:], dsel[:], AX.X, ALU.add).then_inc(S["dest_steps"], 1)
                    dve.wait_ge(S["dest_steps"], 3 * n + 3)
                    v.tensor_copy(dst[:, db, :], dstf[:]).then_inc(S["dest_ready"], 1)
                if r == 6 and live_b(-1):
                    prep_turned((db + 1) % 2, b0 + db + 2)
                if r == 7 and live_b(1):
                    n = b0 + db
                    dve.wait_ge(S["a_tr"], n)
                    stats(lambda t: psM[:, t * P:(t + 1) * P], st2, mv2, S["st2_done"], S["mv2_done"], n)

            dve.wait_ge(S["consts_ready"], 1)
            phases(dve, slot)
            FFN["dve"](dve)

        @block.gpsimd
        def _(pool):
            g = nc.gpsimd

            def inv_sqrt(dst_, ve, src, mv_done, ve_done, done, n):
                pool.wait_ge(mv_done, n)
                g.tensor_tensor(ve[:], src, eps_t[:], ALU.add).then_inc(ve_done, 1)
                pool.wait_ge(ve_done, n)
                g.tensor_tensor(dst_, ve[:], neg_half[:], ALU.pow).then_inc(done, 1)

            steps = ctx.enter_context(nc.semaphore("const_steps"))
            nst = [0]

            def step(ins):
                nst[0] += 1
                ins.then_inc(steps, 1)
                pool.wait_ge(steps, nst[0])

            step(g.memset(neg_half[:], -0.5))
            step(g.memset(eps_t[:], EPS))
            inv_sqrt(rs1[:], ve1, mv1[:, :, 1], S["mv1_done"], S["ve1_done"], S["rs1_done"], 1)
            step(g.memset(ident[:], 0.0))
            step(g.affine_select(ident[:], ident[:], [[-1, P]], ALU.not_equal, 1.0, base=0, channel_multiplier=1))
            step(g.tensor_copy(identb[:], ident[:]))
            step(g.memset(onesb[:], 1.0))
            step(g.memset(maskb[:], 0.0))
            step(g.affine_select(maskb[:], maskb[:], [[-1, P]], ALU.is_ge, MASKED, base=0, channel_multiplier=1))
            step(g.affine_select(before[:], onesb[:], [[1, P]], ALU.is_gt, 0.0, base=0, channel_multiplier=-1))
            step(g.iota(iota_i[:], [[-1, E]], base=E, channel_multiplier=0))
            step(g.tensor_copy(rev_e[:], iota_i[:]))
            step(g.iota(iota_i[:], [[REGION, E]], base=0, channel_multiplier=0))
            step(g.tensor_copy(base[:, 0, :], iota_i[:]))
            step(g.tensor_copy(regb[:], iota_i[:]))
            step(g.iota(tixi[:], [[1, TILES]], base=0, channel_multiplier=0))
            step(g.tensor_copy(tix[:], tixi[:]))
            step(g.memset(padr[:], 0.0))
            g.memset(padr[:, :, C_ID:C_ID + 1].bitcast(U32), NOWHERE).then_inc(S["pads_ready"], 1)
            step(g.iota(iota_i[:, 0:2], [[P, 2]], base=0, channel_multiplier=1))
            g.tensor_copy(idf[:, 0, :], iota_i[:, 0:2]).then_inc(S["consts_ready"], 1)

            def slot(g0, b0, s, live, live_b):
                r, db = s % PAIRS, s // PAIRS
                if live(2):
                    p2 = (s - 2) % 4
                    pool.wait_ge(S["rinv_ready"], g0 + s - 1)
                    for q, (a, z) in enumerate(((0, P), (P, 384))):
                        pr = prob[:, p2, :, a:z]
                        last = g.tensor_tensor(pr, pr, rinv[:, p2, :, q:q + 1].broadcast_to([P, 2, z - a]), ALU.mult)
                    last.then_inc(S["norm_ready"], 1)
                if r == 0 and live_b(2):
                    n = b0 + db - 1
                    pool.wait_ge(S["a_norm"], n)
                    pool.wait_ge(S["xr_loaded"], 16 * n)
                    g.tensor_tensor(pay[:, db, :, 0:P], an[:], xres[:, db], ALU.add).then_inc(S["x1_ready"], 1)
                if r == 1 and live_b(2):
                    n = b0 + db - 2
                    k = [6 * n]

                    def link(ins):
                        k[0] = k[0] + 1
                        ins.then_inc(S["r3_steps"], 1)
                        pool.wait_ge(S["r3_steps"], k[0])

                    rs3 = pay[:, db, :, C_RSTD]
                    pool.wait_ge(S["mv3_done"], n + 1)
                    link(g.tensor_tensor(ve3[:], mv3[:, :, 1], eps_t[:], ALU.add))
                    link(g.tensor_tensor(rs3, ve3[:], neg_half[:], ALU.pow))
                    link(g.tensor_tensor(w3[:, 0, :], mv3[:, :, 1], rs3, ALU.mult))
                    link(g.tensor_tensor(w3[:, 1, :], w3[:, 0, :], rs3, ALU.mult))
                    link(g.tensor_tensor(w3[:, 2, :], w3[:, 1, :], eps_t[:], ALU.add))
                    link(g.tensor_tensor(pay[:, db, :, C_RSTD2], w3[:, 2, :], neg_half[:], ALU.pow))
                if r == 2 and live_b(-1):
                    inv_sqrt(rs1[:], ve1, mv1[:, :, 1], S["mv1_done"], S["ve1_done"], S["rs1_done"], b0 + db + 2)
                if r == 5 and live_b(2):
                    wait_apart(pool, S["dest_ready"], b0 + db - 1)
                    for t in range(2):
                        g.indirect_dma_start(rows, bass.IndirectOffsetOnAxis(ap=dst[:, db, t:t + 1], axis=0),
                                             pay[:, db, t, :], None).then_inc(S["scattered"], 16)
                if r == 7 and live_b(2):
                    pool.wait_ge(S["scattered"], 32 * (b0 + db - 1))
                if r == 7 and live_b(1):
                    inv_sqrt(rs2[:], ve2, mv2[:, :, 1], S["mv2_done"], S["ve2_done"], S["rs2_done"], b0 + db)

            phases(pool, slot)
            FFN["pool"](pool)


def kernel(L0_attn_x, L0_attn_w_kv_down, L0_attn_w_kv_up, L0_attn_w_q, L0_attn_w_out, L0_ffn_centroids,
           L0_ffn_gamma, L0_ffn_beta, L0_ffn_W1, L0_ffn_b1, L0_ffn_W2, L0_ffn_b2):
    import numpy as np
    import concourse.bacc as bacc
    from concourse.bass_utils import run_bass_kernel_spmd

    shape = L0_attn_x.shape
    C = shape[-1]
    HD = L0_attn_w_q.shape[1]
    E, F, _ = L0_ffn_W1.shape
    lay = lambda a, *perm: np.ascontiguousarray(np.transpose(a, perm))
    arrays = {
        "x": np.asarray(L0_attn_x).reshape(-1, C),
        "wd_t": lay(L0_attn_w_kv_down, 1, 0),
        "wup": np.asarray(L0_attn_w_kv_up),
        "wq_t": lay(np.asarray(L0_attn_w_q).reshape(C, HD // P, P), 2, 1, 0),
        "wo": lay(np.asarray(L0_attn_w_out).reshape(HD // P, P, C), 1, 0, 2),
        "cent_t": lay(L0_ffn_centroids, 1, 0),
        "gamma_t": lay(L0_ffn_gamma, 1, 0),
        "beta_t": lay(L0_ffn_beta, 1, 0),
        "ffn_w": np.concatenate([
            lay(L0_ffn_W1, 2, 0, 1),
            lay(np.asarray(L0_ffn_b1).reshape(E, F // P, P), 2, 0, 1),
            lay(np.asarray(L0_ffn_W2).reshape(E, C, F // P, P), 3, 0, 2, 1).reshape(P, E, F),
            lay(L0_ffn_b2, 1, 0).reshape(C, E, 1)], axis=2),
    }
    arrays = {k: np.ascontiguousarray(a) for k, a in arrays.items()}
    nc = bacc.Bacc("TRN2", target_bir_lowering=False, num_devices=1)
    args = [nc.dram_tensor(k, a.shape, mybir.dt.from_np(a.dtype), kind="ExternalInput").ap()
            for k, a in arrays.items()]
    out = nc.dram_tensor("out", arrays["x"].shape, F32, kind="ExternalOutput").ap()
    block_kernel(nc, *args, out)
    r = run_bass_kernel_spmd(nc, [arrays], core_ids=[0])
    return r.results[0]["out"].reshape(shape)
```

```python
from contextlib import ExitStack

import concourse.bass as bass
from concourse import mybir

ALU = mybir.AluOpType
ACT = mybir.ActivationFunctionType
AX = mybir.AxisListType
F32 = mybir.dt.float32
F32R = mybir.dt.float32r
BF16 = mybir.dt.bfloat16
U32 = mybir.dt.uint32
I32 = mybir.dt.int32

P = 128
EPS = 1e-5
MASKED = -3.0e38

C_RSTD = 128
C_SHIFT = 129
C_RSTD2 = 130
C_SCORE = 131
C_ID = 132
ROW = 136
NOWHERE = 1 << 20


def block_kernel(nc, x, wd_t, wup, wq_t, wo, cent_t, gamma_t, beta_t, ffn_w, out):
    ntok, C = x.shape
    T = 256
    NB = ntok // T
    HD = wup.shape[1] // 2
    D = 64
    NH = HD // D
    E = cent_t.shape[1]
    FB = ffn_w.shape[2] // (2 * P)
    PAIRS = NH // 2
    SLOTS = 2 * PAIRS
    ITERS = NB // 2
    PAD = 2 * T
    REGION = ntok + T
    TILES = ntok // T + E - 1
    TILES += -TILES % 8
    assert C == P and PAIRS == 8 and NB % 2 == 0 and ITERS >= 2

    rows = nc.dram_tensor("routed_rows", [E * REGION + T, ROW], F32, kind="Internal").ap()

    with ExitStack() as ctx:
        def sb(name, shape, dt=F32):
            return ctx.enter_context(nc.sbuf_tensor(name, shape, dt))

        def ps(name, shape, dt=F32):
            return ctx.enter_context(nc.psum_tensor(name, shape, dt))

        def sem(name):
            return ctx.enter_context(nc.semaphore(name))

        psT = ps("psT", [P, 2, T])
        psS = ps("psS", [P, 2, 512])
        psP = ps("psP", [P, 2, 512])
        psZU = ps("psZU", [P, 2, 512])
        psZ = psZU[:, 0, :].rearrange("p (h q) -> p h q", h=2)
        psU = psZU[:, 1, :]
        psM = ps("psM", [P, 512])
        psAB = (psP[:, :, 0:2 * P], psZU[:, :, 0:2 * P])

        ab_hi = sb("ab_hi", [P, NH, 2, P], F32R)
        ab_lo = sb("ab_lo", [P, NH, 2, P], F32R)
        cent = sb("cent", [P, E])
        gam = sb("gam", [P, E])
        bet = sb("bet", [P, E])
        wx = sb("wx", [P, E, 2 * FB * P + FB + 1])
        B1, W2 = FB * P, FB * P + FB

        ident = sb("ident", [P, P])
        mask = sb("mask", [P, 384])
        before = sb("before", [P, P], BF16)
        onesb = sb("onesb", [P, P], BF16)
        neg_half = sb("neg_half", [P, 2])
        eps_t = sb("eps_t", [P, 2])
        rev_e = sb("rev_e", [P, E])
        iota_i = sb("iota_i", [P, E], I32)

        xin = sb("xin", [P, 2, 2, P])
        xres = sb("xres", [P, 2, 2, P])
        st1 = sb("st1", [P, 2, 6])
        mv1 = sb("mv1", [P, 2, 2])
        ve1 = sb("ve1", [P, 2])
        rs1 = sb("rs1", [P, 2])
        xn = sb("xn", [P, 2, P])
        xk_hi = sb("xk_hi", [P, 2, 2, P], F32R)
        xk_lo = sb("xk_lo", [P, 2, 2, P], F32R)
        xt_hi = sb("xt_hi", [P, 2, T], F32R)
        xt_lo = sb("xt_lo", [P, 2, T], F32R)
        t_hi = sb("t_hi", [P, 2, 2, T], F32R)
        t_lo = sb("t_lo", [P, 2, 2, T], F32R)
        nmax = sb("nmax", [P, 4, 2, 2])
        rsum = sb("rsum", [P, 4, 2, 2])
        rinv = sb("rinv", [P, 4, 2, 2])
        nscore = sb("nscore", [P, 2, 384])
        prob = sb("prob", [P, 4, 2, 384])
        p_hi = sb("p_hi", [P, 2, 2, 384], F32R)
        p_lo = sb("p_lo", [P, 2, 2, 384], F32R)
        z_hi = sb("z_hi", [P, 2, 2, T], F32R)
        z_lo = sb("z_lo", [P, 2, 2, T], F32R)
        at = sb("at", [P, T])
        st2 = sb("st2", [P, 2, 6])
        mv2 = sb("mv2", [P, 2, 2])
        ve2 = sb("ve2", [P, 2])
        rs2 = sb("rs2", [P, 2])
        an = sb("an", [P, 2, P])
        pay = sb("pay", [P, 2, 2, ROW])
        st3 = sb("st3", [P, 2, 6])
        mv3 = sb("mv3", [P, 2, 2])
        ve3 = sb("ve3", [P, 2])
        w3 = sb("w3", [P, 3, 2])
        fn = sb("fn", [P, 2, P])
        ft = sb("ft", [P, T])
        hits = sb("hits", [P, 2, E])
        hitr = sb("hitr", [P, 2, E])
        first = sb("first", [P, 2])
        oh = sb("oh", [P, 2, E], BF16)
        base = sb("base", [P, 2, E])
        dsum = sb("dsum", [P, 2, E])
        dsel = sb("dsel", [P, 2, E])
        dstf = sb("dstf", [P, 2])
        dst = sb("dst", [P, 2, 2], U32)
        idf = sb("idf", [P, 2, 2])

        wd_s = sb("wd_s", [P, P])
        wup_s = sb("wup_s", [P, 2 * HD])
        wq_s = sb("wq_s", [P, HD // P, P])
        wo_s = sb("wo_s", [P, HD // P, P])
        kv_t = sb("kv_t", [P, 2, HD // P, P])

        names = """w_loaded qo_loaded ffnw_loaded consts_ready kv_done kv_copied ab_done ab_hi_done ab_split
            bias_done bias_added weights_ready
            x_loaded xr_loaded st1_done mv1_done ve1_done rs1_done xn_ready xk_hi_done xn_tr xt_hi_done x_split xk_split
            t_ready t_hi_done t_split s_ready nmax_ready probs_ready rinv_ready norm_ready pt_ready p_hi_done p_split
            z_ready z_hi_done z_split u_done u_copied a_tr st2_done mv2_done ve2_done rs2_done a_norm x1_ready
            st3_done mv3_done r3_steps f_ready f_tr ft_ready scored argmax_steps onehot_ready ranked dest_steps
            dest_ready scattered"""
        S = {n: sem(n) for n in names.split()}
        FU = 8
        W1W = FB * P + FB
        WW = W1W + FB * P + 1
        regb = sb("regb", [P, E])
        padr = sb("padr", [P, PAD // P, ROW])
        cnt = sb("cnt", [P, E])
        cnti = sb("cnti", [P, 2, E], I32)
        ends = sb("ends", [P, E], I32)
        ntile = sb("ntile", [P, E])
        csum = sb("csum", [P, 3, E])
        tix = sb("tix", [P, TILES])
        tixi = sb("tixi", [P, TILES], I32)
        past = sb("past", [P, TILES, E])
        pastn = sb("pastn", [P, TILES, E])
        texp = sb("texp", [P, TILES])
        tpre = sb("tpre", [P, TILES])
        trow = sb("trow", [P, 3, TILES])
        table = sb("table", [P, TILES, 2], I32)
        fin = sb("fin", [P, FU, 2, ROW])
        ff = sb("ff", [P, FU, 2, P])
        nn = sb("nn", [P, 2, P])
        nt = sb("nt", [P, 2, T])
        wst = sb("wst", [P, 4, WW])
        assert 2 * HD == 2 * FB * T
        hid = wup_s[:].rearrange("p (b j t) -> p b j t", b=2, j=FB)
        yt = sb("yt", [P, T])
        ea = sb("ea", [P, FU, 2])
        ea1 = sb("ea1", [P, 2])
        alpha = sb("alpha", [P, FU, 2])
        gg = sb("gg", [P, 2, 2, P])
        gst = sb("gst", [P, 2, 6])
        carry = sb("carry", [P, 1])
        gmv = sb("gmv", [P, 2, 2, 2])
        gve = sb("gve", [P, 2])
        grs = sb("grs", [P, 2, 2])
        on = sb("on", [P, 2, P])
        res = sb("res", [P, 2, 2, P])
        for n in """pads_ready pad_stored spare_stored ends_ready table_steps table_ready wst_ready exp_done nt_ready
            relu_a relu_d ff_done nn_ready n_tr h_done yt_done yt_ready y_tr alpha_steps g_steps gmv_ready gve_done
            grs_ready on_ready res_ready""".split():
            S[n] = sem(n)
        f_loaded = [sem(f"f_loaded{i}") for i in range(FU)]
        stored = [sem(f"stored{i}") for i in range(FU)]
        psH = psS[:].rearrange("p b (j t) -> p (b j) t", j=2)
        psN, psY, psO = psU, psT, psZ

        def ffn_phases(eng, slot):
            for s in range(FU):
                slot(0, 0, s, lambda lag: s >= lag)
            with eng.Fori(1, TILES // FU) as it:
                m0 = eng.snap(it * FU)
                n0 = eng.snap(it * 16)
                for s in range(FU):
                    slot(m0, n0, s, lambda lag: True)
            for s in range(5):
                slot(TILES, TILES // FU * 16, s, lambda lag: s < lag)

        def pad(eng, experts):
            eng.wait_ge(S["ends_ready"], 1)
            for e in experts:
                row = eng.value_load(ends[0:1, e:e + 1], min_val=0, max_val=(e + 1) * REGION - PAD)
                eng.dma_start(rows[bass.ds(row, PAD), :].rearrange("(t p) c -> p t c", p=P),
                              padr[:]).then_inc(S["pad_stored"], 16)

        def ffn_sp(sp):
            sp.wait_ge(S["table_ready"], 1)

            def slot(m0, n0, s, live):
                if not live(0):
                    return
                if live(FU):
                    sp.wait_ge(stored[s], n0 + n0)
                row = sp.value_load(table[0:1, bass.ds(m0 + s, 1), 0], min_val=0, max_val=E * REGION)
                if s == 0 and not live(FU):
                    sp.wait_ge(S["scattered"], 32 * NB)
                    sp.wait_ge(S["pad_stored"], 16 * E)
                    sp.wait_ge(S["spare_stored"], 16)
                sp.dma_start(fin[:, s], rows[bass.ds(row, T), :].rearrange("(t p) c -> p t c", p=P)
                             ).then_inc(f_loaded[s], 16)

            ffn_phases(sp, slot)

        def ffn_pe(pe):
            mm = nc.tensor.matmul

            def slot(m0, n0, s, live):
                if live(1):
                    pe.wait_ge(S["nt_ready"], m0 + s)
                    pe.wait_ge(S["wst_ready"], m0 + s)
                    if live(2):
                        pe.wait_ge(S["relu_a"], m0 + s - 1)
                        pe.wait_ge(S["relu_d"], m0 + s - 1)
                    for j in range(FB):
                        last = mm(psH[:, j, :], wst[:, (s - 1) % 4, j * P:(j + 1) * P], nt[:, (s - 1) % 2, :],
                                  start=True, stop=True)
                    last.then_inc(S["h_done"], 1)
                if live(3):
                    pe.wait_ge(S["yt_ready"], m0 + s - 2)
                    if live(4):
                        pe.wait_ge(S["g_steps"], 2 * (m0 + s - 3))
                    for t in range(2):
                        last = nc.tensor.transpose(psO[:, t, 0:P], yt[:, t * P:(t + 1) * P], ident[:])
                    last.then_inc(S["y_tr"], 1)
                if live(0):
                    pe.wait_ge(S["nn_ready"], m0 + s + 1)
                    if live(1):
                        pe.wait_ge(S["nt_ready"], m0 + s)
                    for t in range(2):
                        last = nc.tensor.transpose(psN[:, t * P:(t + 1) * P], nn[:, t, :], ident[:])
                    last.then_inc(S["n_tr"], 1)
                if live(2):
                    pe.wait_ge(S["relu_a"], m0 + s - 1)
                    pe.wait_ge(S["relu_d"], m0 + s - 1)
                    if live(3):
                        pe.wait_ge(S["yt_ready"], m0 + s - 2)
                    for j in range(FB):
                        a = W1W + j * P
                        last = mm(psY[:, 0, :], wst[:, (s - 2) % 4, a:a + P], hid[:, s % 2, j, :],
                                  start=(j == 0), stop=(j == FB - 1))
                    last.then_inc(S["yt_done"], 1)

            ffn_phases(pe, slot)

        def ffn_act(act):
            act.wait_ge(S["table_ready"], 1)
            act.wait_ge(S["bias_added"], 1)
            act.wait_ge(S["weights_ready"], 1)

            def slot(m0, n0, s, live):
                if live(0):
                    if live(4):
                        act.wait_ge(S["yt_done"], m0 + s - 3)
                        act.wait_ge(S["yt_ready"], m0 + s - 3)
                        act.wait_ge(S["relu_d"], m0 + s - 3)
                    e = act.value_load(table[0:1, bass.ds(m0 + s, 1), 1], min_val=0, max_val=E - 1)
                    nc.scalar.activation(wst[:, s % 4, :], wx[:, bass.ds(e, 1), :].rearrange("p a c -> p (a c)"),
                                         ACT.Copy).then_inc(S["wst_ready"], 1)
                    act.wait_ge(f_loaded[s], n0 + 16)
                    nc.scalar.activation(ea[:, s, :], fin[:, s, :, C_SCORE], ACT.Exp,
                                         scale=-1.0).then_inc(S["exp_done"], 1)
                    act.wait_ge(S["n_tr"], m0 + s + 1)
                    if live(2):
                        act.wait_ge(S["h_done"], m0 + s - 1)
                    nc.scalar.activation(nt[:, s % 2, :], psN[:, 0:T], ACT.Copy).then_inc(S["nt_ready"], 1)
                if live(1):
                    act.wait_ge(S["h_done"], m0 + s)
                    if live(3):
                        act.wait_ge(S["yt_done"], m0 + s - 2)
                    w = wst[:, (s - 1) % 4, :]
                    for j in range(2):
                        last = nc.scalar.activation(hid[:, (s - 1) % 2, j, :], psH[:, j, :], ACT.Relu,
                                                    bias=w[:, FB * P + j:FB * P + j + 1])
                    last.then_inc(S["relu_a"], 1)
                if live(2):
                    act.wait_ge(S["yt_done"], m0 + s - 1)
                    if live(3):
                        act.wait_ge(S["y_tr"], m0 + s - 2)
                    nc.scalar.activation(yt[:], psY[:, 0, :], ACT.Identity,
                                         bias=wst[:, (s - 2) % 4, WW - 1:WW]).then_inc(S["yt_ready"], 1)

            ffn_phases(act, slot)

        def ffn_dve(dve):
            v = nc.vector
            k = [0]

            def link(ins):
                k[0] += 1
                ins.then_inc(S["table_steps"], 1)
                dve.wait_ge(S["table_steps"], k[0])

            dve.wait_ge(S["dest_ready"], NB)
            last_base = base[:, NB % 2, :]
            link(v.tensor_tensor(cnt[:], last_base, regb[:], ALU.subtract))
            link(v.tensor_scalar(cnti[:, 0, :], cnt[:], float(T - 1), None, ALU.add))
            link(v.tensor_single_scalar(cnti[:, 1, :], cnti[:, 0, :], 8, ALU.arith_shift_right))
            link(v.tensor_copy(ntile[:], cnti[:, 1, :]))
            src = ntile[:]
            for n, d in enumerate((1, 2, 4)):
                v.tensor_copy(csum[:, n, 0:d], src[:, 0:d])
                link(v.tensor_tensor(csum[:, n, d:E], src[:, d:E], src[:, 0:E - d], ALU.add))
                src = csum[:, n, :]
            link(v.tensor_tensor(past[:], tix[:].unsqueeze(2).broadcast_to([P, TILES, E]),
                                 src.unsqueeze(1).broadcast_to([P, TILES, E]), ALU.is_ge))
            v.tensor_reduce(texp[:], past[:], AX.X, ALU.add)
            link(v.tensor_tensor(pastn[:], past[:], ntile[:].unsqueeze(1).broadcast_to([P, TILES, E]), ALU.mult))
            link(v.tensor_reduce(tpre[:], pastn[:], AX.X, ALU.add))
            link(v.tensor_tensor(trow[:, 0, :], tix[:], tpre[:], ALU.subtract))
            link(v.tensor_scalar(trow[:, 1, :], trow[:, 0, :], float(T), None, ALU.mult))
            link(v.scalar_tensor_tensor(trow[:, 2, :], texp[:], float(REGION), trow[:, 1, :], ALU.mult, ALU.add))
            v.tensor_scalar(table[:, :, 0], trow[:, 2, :], float(E * REGION), None, ALU.min)
            v.tensor_scalar(table[:, :, 1], texp[:], float(E - 1), None, ALU.min).then_inc(S["table_ready"], 1)

            def slot(m0, n0, s, live):
                if live(0):
                    dve.wait_ge(f_loaded[s], n0 + 16)
                    for t in range(2):
                        last = v.tensor_scalar(ff[:, s, t, :], fin[:, s, t, 0:P], fin[:, s, t, C_RSTD:C_RSTD + 1],
                                               fin[:, s, t, C_SHIFT:C_SHIFT + 1], ALU.mult, ALU.add)
                    last.then_inc(S["ff_done"], 1)
                if live(0):
                    dve.wait_ge(S["ff_done"], m0 + s + 1)
                    if live(1):
                        dve.wait_ge(S["n_tr"], m0 + s)
                    for t in range(2):
                        last = v.tensor_scalar(nn[:, t, :], ff[:, s, t, :], fin[:, s, t, C_RSTD2:C_RSTD2 + 1], None,
                                               ALU.mult)
                    last.then_inc(S["nn_ready"], 1)
                if live(1):
                    dve.wait_ge(S["h_done"], m0 + s)
                    if live(3):
                        dve.wait_ge(S["yt_done"], m0 + s - 2)
                    w = wst[:, (s - 1) % 4, :]
                    for j in range(2, FB):
                        last = v.tensor_scalar(hid[:, (s - 1) % 2, j, :], psH[:, j, :],
                                               w[:, FB * P + j:FB * P + j + 1], 0.0, ALU.add, ALU.max)
                    last.then_inc(S["relu_d"], 1)
                if live(4):
                    b = s % 2
                    dve.wait_ge(S["grs_ready"], m0 + s - 3)
                    if live(5):
                        dve.wait_ge(S["res_ready"], m0 + s - 4)
                    for t in range(2):
                        last = v.tensor_scalar(on[:, t, :], gg[:, b, t, :], gmv[:, b, t, 0:1], grs[:, b, t:t + 1],
                                               ALU.subtract, ALU.mult)
                    last.then_inc(S["on_ready"], 1)
                if live(3):
                    b, sf = (s - 3) % 2, (s - 3) % FU
                    m = m0 + s - 3
                    dve.wait_ge(S["y_tr"], m + 1)
                    for t in range(2):
                        last = v.scalar_tensor_tensor(gg[:, b, t, :], psO[:, t, 0:P], alpha[:, sf, t:t + 1],
                                                      ff[:, sf, t, :], ALU.mult, ALU.add)
                    last.then_inc(S["g_steps"], 1)
                if live(3):
                    dve.wait_ge(S["g_steps"], 2 * m + 1)
                    for t in range(2):
                        last = v.bn_stats(gst[:, t, :], gg[:, b, t, :])
                    last.then_inc(S["g_steps"], 1)
                if live(0):
                    dve.wait_ge(S["exp_done"], m0 + s + 1)
                    v.tensor_scalar(ea1[:], ea[:, s, :], 1.0, None, ALU.add).then_inc(S["alpha_steps"], 1)
                if live(3):
                    dve.wait_ge(S["g_steps"], 2 * m + 2)
                    v.tensor_copy(carry[:], gst[:, 0, 0:1])
                    for t in range(2):
                        last = v.bn_aggr(gmv[:, b, t, :], gst[:, t, :])
                    last.then_inc(S["gmv_ready"], 1)
                if live(0):
                    dve.wait_ge(S["alpha_steps"], m0 + s + 1)
                    v.reciprocal(alpha[:, s, :], ea1[:])

            ffn_phases(dve, slot)

        def ffn_pool(pool):
            g = nc.gpsimd

            def slot(m0, n0, s, live):
                if live(4):
                    m, b, sf = m0 + s - 4, (s - 4) % 2, (s - 4) % FU
                    pool.wait_ge(S["on_ready"], m + 1)
                    if live(6):
                        pool.wait_ge(stored[(s - 6) % FU], n0 + n0 + (32 if s >= 6 else 0))
                    g.tensor_tensor(res[:, b], on[:], fin[:, sf, :, 0:P], ALU.add).then_inc(S["res_ready"], 1)
                if live(3):
                    m3, b3 = m0 + s - 3, (s - 3) % 2
                    pool.wait_ge(S["gmv_ready"], m3 + 1)
                    g.tensor_tensor(gve[:], gmv[:, b3, :, 1], eps_t[:], ALU.add).then_inc(S["gve_done"], 1)
                    pool.wait_ge(S["gve_done"], m3 + 1)
                    g.tensor_tensor(grs[:, b3, :], gve[:], neg_half[:], ALU.pow).then_inc(S["grs_ready"], 1)
                if live(4):
                    wait_apart(pool, S["res_ready"], m + 1)
                    for t in range(2):
                        g.indirect_dma_start(out, bass.IndirectOffsetOnAxis(
                            ap=fin[:, sf, t, C_ID:C_ID + 1].bitcast(U32), axis=0), res[:, b, t, :], None,
                            bounds_check=ntok - 1, oob_is_err=False).then_inc(stored[sf], 16)

            ffn_phases(pool, slot)
            for i in range(FU):
                pool.wait_ge(stored[i], TILES // FU * 32)

        FFN = {"sp": ffn_sp, "pe": ffn_pe, "act": ffn_act, "dve": ffn_dve, "pool": ffn_pool}
        block = ctx.enter_context(nc.Block())

        def wait_apart(eng, what, value):
            if not isinstance(value, int):
                eng.compute_val(value)
            eng.wait_ge(S["x_loaded"], 16)
            eng.wait_ge(what, value)

        AB_SLOTS = HD // P // 2 - 1

        def setup_slot(s, live):
            return s < AB_SLOTS and not live(s + 1)

        def phases(eng, slot):
            for s in range(SLOTS):
                slot(0, 0, s, lambda lag: s >= lag, lambda d: s // PAIRS >= d)
            if ITERS > 2:
                with eng.Fori(1, ITERS - 1) as it:
                    g0 = eng.snap(it * SLOTS)
                    b0 = eng.snap(it * 2)
                    for s in range(SLOTS):
                        slot(g0, b0, s, lambda lag: True, lambda d: True)
            for s in range(SLOTS):
                slot((ITERS - 1) * SLOTS, NB - 2, s, lambda lag: True,
                     lambda d: s // PAIRS - d < 2)
            for s in range(SLOTS):
                slot(ITERS * SLOTS, NB, s, lambda lag: s < lag, lambda d: s // PAIRS < d)

        @block.sync
        def _(sp):
            for dst_, src in ((wd_s[:], wd_t), (wup_s[:], wup)):
                sp.dma_start(dst_, src).then_inc(S["w_loaded"], 16)

            def load_x(buf, bpar, b, done):
                src = x[bass.ds(b * T, T), :].rearrange("(t p) c -> p t c", p=P)
                sp.dma_start(buf[:, bpar], src).then_inc(done, 16)

            load_x(xin, 0, 0, S["x_loaded"])
            for dst_, src in ((wq_s[:], wq_t), (wo_s[:], wo)):
                sp.dma_start(dst_, src).then_inc(S["qo_loaded"], 16)
            for dst_, src in ((cent[:], cent_t), (gam[:], gamma_t), (bet[:], beta_t),
                              (wx[:, 0:E // 2], ffn_w[:, 0:E // 2]), (wx[:, E // 2:], ffn_w[:, E // 2:])):
                sp.dma_start(dst_, src).then_inc(S["ffnw_loaded"], 16)

            def slot(g0, b0, s, live, live_b):
                r, db = s % PAIRS, s // PAIRS
                if r == 0 and live_b(-1):
                    sp.wait_ge(S["xn_ready"], b0 + db + 1)
                    load_x(xin, (db + 1) % 2, b0 + db + 1, S["x_loaded"])
                if r == 3 and live_b(1):
                    if live_b(2):
                        sp.wait_ge(S["x1_ready"], b0 + db - 1)
                    load_x(xres, (db - 1) % 2, b0 + db - 1, S["xr_loaded"])
                if not live(0) and s == 6:
                    pad(sp, range(0, E // 2))

            sp.wait_ge(S["pads_ready"], 1)
            sp.dma_start(rows[E * REGION:E * REGION + T, :].rearrange("(t p) c -> p t c", p=P),
                         padr[:, 0:2]).then_inc(S["spare_stored"], 16)
            phases(sp, slot)
            FFN["sp"](sp)

        @block.tensor
        def _(pe):
            mm = nc.tensor.matmul
            pe.wait_ge(S["w_loaded"], 32)
            for j in range(HD // P):
                if j >= 2:
                    pe.wait_ge(S["kv_copied"], j - 1)
                for kv in range(2):
                    last = mm(psS[:, j % 2, kv * P:(kv + 1) * P],
                              wup_s[:, kv * HD + j * P:kv * HD + (j + 1) * P], wd_s[:], start=True, stop=True)
                last.then_inc(S["kv_done"], 1)
            pe.wait_ge(S["qo_loaded"], 32)
            def head_matrices(j):
                pe.wait_ge(S["kv_copied"], j + 1)
                if j >= 2:
                    pe.wait_ge(S["ab_split"], j - 1)
                for e in range(2):
                    h = slice(64 * e, 64 * e + 64)
                    mm(psAB[j % 2][:, e, 0:P], wq_s[h, j, :], kv_t[h, 0, j, :], start=True, stop=True)
                    last = mm(psAB[j % 2][:, e, P:2 * P], kv_t[h, 1, j, :], wo_s[h, j, :], start=True, stop=True)
                last.then_inc(S["ab_done"], 1)

            head_matrices(0)
            head_matrices(1)

            def turn_x():
                for t in range(2):
                    last = nc.tensor.transpose(psM[:, t * P:(t + 1) * P], xn[:, t, :], ident[:])
                last.then_inc(S["xn_tr"], 1)

            pe.wait_ge(S["consts_ready"], 1)
            pe.wait_ge(S["xn_ready"], 1)
            turn_x()

            def first_bias(experts):
                for e in experts:
                    for j in range(FB):
                        last = mm(psT[:, 0, e * FB + j:e * FB + j + 1], wx[:, e, j * P:(j + 1) * P], bet[:, e:e + 1],
                                  start=True, stop=True)
                last.then_inc(S["bias_done"], 1)

            def scores(h, tb, xb, freed):
                if freed is not None:
                    pe.wait_ge(S["nmax_ready"], freed)
                terms = ((t_lo, xt_hi), (t_hi, xt_lo), (t_hi, xt_hi))
                for q, (a, z) in enumerate(((0, P), (P, 384))):
                    for n, (tt, xx) in enumerate(terms):
                        last = mm(psS[:, h, a:z], tt[:, tb, h, q * P:(q + 1) * P], xx[:, xb, 0:z - a],
                                  start=(n == 0), stop=(n == 2))
                last.then_inc(S["s_ready"], 1)

            def slot(g0, b0, s, live, live_b):
                r, db = s % PAIRS, s // PAIRS
                if live(0):
                    if r == 0:
                        pe.wait_ge(S["x_split"], b0 + db + 1)
                    if live(1):
                        pe.wait_ge(S["t_split"], g0 + s)
                    if not live(s + 1) and s <= AB_SLOTS:
                        pe.wait_ge(S["ab_split"], s + 1 if s < AB_SLOTS else HD // P)
                    for h in range(2):
                        hh = 2 * r + h
                        mm(psT[:, h, :], ab_lo[:, hh, 0, :], xt_hi[:, db, :], start=True, stop=False)
                        mm(psT[:, h, :], ab_hi[:, hh, 0, :], xt_lo[:, db, :], start=False, stop=False)
                        last = mm(psT[:, h, :], ab_hi[:, hh, 0, :], xt_hi[:, db, :], start=False, stop=True)
                    last.then_inc(S["t_ready"], 1)
                if live(3):
                    p3 = (s - 3) % 4
                    pe.wait_ge(S["norm_ready"], g0 + s - 2)
                    if live(4):
                        pe.wait_ge(S["p_split"], g0 + s - 3)
                    for h in range(2):
                        for k in range(3):
                            last = nc.tensor.transpose(psP[:, h, k * P:(k + 1) * P],
                                                       prob[:, p3, h, k * P:(k + 1) * P], ident[:])
                    last.then_inc(S["pt_ready"], 1)
                if setup_slot(s, live):
                    head_matrices(2 * s + 2)
                    head_matrices(2 * s + 3)
                if live(1):
                    pe.wait_ge(S["t_split"], g0 + s)
                    xb = ((s - 1) // PAIRS) % 2
                    for h in range(2):
                        scores(h, (s - 1) % 2, xb, 2 * (g0 + s - 2) + 1 + h if live(2) else None)
                if live(4):
                    zb, zx = (s - 4) % 2, ((s - 4) // PAIRS) % 2
                    pe.wait_ge(S["p_split"], g0 + s - 3)
                    if (s - 4) % PAIRS == 0:
                        pe.wait_ge(S["xk_split"], b0 + (s - 4) // PAIRS + 1)
                    if live(5):
                        pe.wait_ge(S["z_split"], g0 + s - 4)
                    terms = ((xk_lo, p_hi), (xk_hi, p_lo), (xk_hi, p_hi))
                    for n, (xx, pp) in enumerate(terms):
                        mm(psZ[:, :, :], xx[:, zx, 0, :], pp[:, zb, :, 0:T], start=(n == 0), stop=False,
                           skip_group_check=True)
                    for n, (xx, pp) in enumerate(terms):
                        last = mm(psZ[:, :, P:T], xx[:, zx, 1, :], pp[:, zb, :, T:384], start=False, stop=(n == 2),
                                  skip_group_check=True)
                    last.then_inc(S["z_ready"], 1)
                if live(5):
                    ub, ur = (s - 5) % 2, (s - 5) % PAIRS
                    pe.wait_ge(S["z_split"], g0 + s - 4)
                    if ur == 0 and live(5 + PAIRS):
                        pe.wait_ge(S["u_copied"], b0 + (s - 5) // PAIRS)
                    for h in range(2):
                        hh = 2 * ur + h
                        for n, (bb, zz) in enumerate(((ab_lo, z_hi), (ab_hi, z_lo), (ab_hi, z_hi))):
                            last = mm(psU[:, 0:T], bb[:, hh, 1, :], zz[:, ub, h, :],
                                      start=(ur == 0 and h == 0 and n == 0),
                                      stop=(ur == PAIRS - 1 and h == 1 and n == 2))
                    last.then_inc(S["u_done"], 1)
                if s == SLOTS - 1 and not live_b(2):
                    pe.wait_ge(S["ffnw_loaded"], 5 * 16)
                if not live(0) and 1 <= s <= E // 2:
                    first_bias(range(s - 1, s))
                if not live(0) and s == 7:
                    first_bias(range(E // 2, E))
                if r == 2 and live_b(2):
                    pe.wait_ge(S["f_ready"], b0 + db - 1)
                    for t in range(2):
                        last = nc.tensor.transpose(psM[:, t * P:(t + 1) * P], fn[:, t, :], ident[:])
                    last.then_inc(S["f_tr"], 1)
                if r == 3 and live_b(2):
                    pe.wait_ge(S["ft_ready"], b0 + db - 1)
                    for t in range(2):
                        last = mm(psM[:, t * E:(t + 1) * E], ft[:, t * P:(t + 1) * P], cent[:], start=True, stop=True)
                    last.then_inc(S["scored"], 1)
                if r == 4 and live_b(2):
                    pe.wait_ge(S["onehot_ready"], b0 + db - 1)
                    mm(psM[:, 0:E], before[:], oh[:, 0, :], start=True, stop=True)
                    mm(psM[:, E:2 * E], before[:], oh[:, 1, :], start=True, stop=False)
                    mm(psM[:, E:2 * E], onesb[:], oh[:, 0, :], start=False, stop=True)
                    mm(psM[:, 2 * E:3 * E], onesb[:], oh[:, 0, :], start=True, stop=False)
                    mm(psM[:, 2 * E:3 * E], onesb[:], oh[:, 1, :], start=False, stop=True).then_inc(S["ranked"], 1)
                if r == 5 and live_b(-1):
                    pe.wait_ge(S["xn_ready"], b0 + db + 2)
                    if live_b(2):
                        pe.wait_ge(S["dest_ready"], b0 + db - 1)
                    turn_x()
                if r == 6 and live_b(1):
                    pe.wait_ge(S["u_copied"], b0 + db)
                    if live_b(-1):
                        pe.wait_ge(S["x_split"], b0 + db + 2)
                    elif live_b(2):
                        pe.wait_ge(S["dest_ready"], b0 + db - 1)
                    for t in range(2):
                        last = nc.tensor.transpose(psM[:, t * P:(t + 1) * P], at[:, t * P:(t + 1) * P], ident[:])
                    last.then_inc(S["a_tr"], 1)

            phases(pe, slot)
            FFN["pe"](pe)

        @block.scalar
        def _(act):
            cp = lambda o, i: nc.scalar.activation(o, i, ACT.Copy)
            for j in range(HD // P):
                act.wait_ge(S["kv_done"], j + 1)
                nc.scalar.activation(kv_t[:, 0, j, :], psS[:, j % 2, 0:P], ACT.Copy, scale=float(D) ** -0.5)
                cp(kv_t[:, 1, j, :], psS[:, j % 2, P:2 * P]).then_inc(S["kv_copied"], 1)
            def matrices_top(j):
                act.wait_ge(S["ab_done"], j + 1)
                cp(ab_hi[:, 2 * j:2 * j + 2].rearrange("p h m c -> p h (m c)"),
                   psAB[j % 2]).then_inc(S["ab_hi_done"], 1)

            matrices_top(0)
            matrices_top(1)

            def xt_top(par):
                cp(xt_hi[:, par, :], psM[:, 0:T]).then_inc(S["xt_hi_done"], 1)

            act.wait_ge(S["xn_tr"], 1)
            xt_top(0)

            def slot(g0, b0, s, live, live_b):
                r, db = s % PAIRS, s // PAIRS
                def exps(h):
                    p1 = (s - 1) % 4
                    act.wait_ge(S["nmax_ready"], 2 * (g0 + s - 1) + 1 + h)
                    for q, (a, z) in enumerate(((0, P), (P, 384))):
                        last = nc.scalar.activation(prob[:, p1, h, a:z], nscore[:, h, a:z], ACT.Exp,
                                                    bias=nmax[:, p1, h, q:q + 1], scale=-1.0,
                                                    accum_out=rsum[:, p1, h, q:q + 1])
                    last.then_inc(S["probs_ready"], 1)

                if r == 3 and live_b(2):
                    act.wait_ge(S["f_tr"], b0 + db - 1)
                    cp(ft[:], psM[:, 0:T]).then_inc(S["ft_ready"], 1)
                if r == 5 and live_b(1):
                    act.wait_ge(S["u_done"], PAIRS * (b0 + db))
                    if live_b(2):
                        act.wait_ge(S["a_tr"], b0 + db - 1)
                    cp(at[:], psU[:, 0:T]).then_inc(S["u_copied"], 1)
                if r == 6 and live_b(-1):
                    act.wait_ge(S["xn_tr"], b0 + db + 2)
                    if live_b(1):
                        act.wait_ge(S["s_ready"], 2 * PAIRS * (b0 + db))
                    xt_top((db + 1) % 2)
                if not live(0) and s == 6:
                    pad(act, range(E // 2, E))
                if not live(0) and s == 7:
                    act.wait_ge(S["bias_done"], E // 2 + 1)
                    for e in range(E):
                        last = nc.scalar.activation(wx[:, e, 0:FB * P], wx[:, e, 0:FB * P], ACT.Copy,
                                                    scale=gam[:, e:e + 1])
                    last.then_inc(S["weights_ready"], 1)
                if live(0):
                    act.wait_ge(S["t_ready"], g0 + s + 1)
                    if live(2):
                        act.wait_ge(S["s_ready"], 2 * (g0 + s - 1))
                    cp(t_hi[:, s % 2], psT[:]).then_inc(S["t_hi_done"], 1)
                if live(3):
                    act.wait_ge(S["pt_ready"], g0 + s - 2)
                    if live(5):
                        act.wait_ge(S["z_ready"], g0 + s - 4)
                    cp(p_hi[:, (s - 3) % 2], psP[:, :, 0:384]).then_inc(S["p_hi_done"], 1)
                if setup_slot(s, live):
                    matrices_top(2 * s + 2)
                    matrices_top(2 * s + 3)
                if live(1):
                    exps(0)
                if live(4):
                    act.wait_ge(S["z_ready"], g0 + s - 3)
                    if live(6):
                        act.wait_ge(S["u_done"], g0 + s - 5)
                    cp(z_hi[:, (s - 4) % 2], psZ[:]).then_inc(S["z_hi_done"], 1)
                if live(1):
                    exps(1)

            phases(act, slot)
            FFN["act"](act)

        @block.vector
        def _(dve):
            v = nc.vector

            def stats(src, st, st_done):
                for t in range(2):
                    last = v.bn_stats(st[:, t, :], src(t))
                last.then_inc(st_done, 1)

            def aggregate(st, mv, st_done, mv_done, n):
                wait_apart(dve, st_done, n)
                for t in range(2):
                    last = v.bn_aggr(mv[:, t, :], st[:, t, :])
                last.then_inc(mv_done, 1)

            def normalise(dst_, src, mv, rs, done):
                for t in range(2):
                    last = v.tensor_scalar(dst_(t), src(t), mv[:, t, 0:1], rs(t), ALU.subtract, ALU.mult)
                last.then_inc(done, 1)

            def prep_stats(par, n):
                dve.wait_ge(S["x_loaded"], 16 * n)
                stats(lambda t: xin[:, par, t, :], st1, S["st1_done"])

            def prep_norm(par, n, reuse):
                dve.wait_ge(S["rs1_done"], n)
                if reuse is not None:
                    dve.wait_ge(S["xn_tr"], reuse)
                    dve.wait_ge(S["xk_split"], reuse)
                normalise(lambda t: xn[:, t, :], lambda t: xin[:, par, t, :], mv1,
                          lambda t: rs1[:, t:t + 1], S["xn_ready"])

            def prep_turned(par, n):
                dve.wait_ge(S["xt_hi_done"], n)
                v.tensor_tensor(xt_lo[:, par, :], psM[:, 0:T], xt_hi[:, par, :].bitcast(F32),
                                ALU.subtract).then_inc(S["x_split"], 1)

            dve.memset(pay[:], 0.0)
            prep_stats(0, 1)
            aggregate(st1, mv1, S["st1_done"], S["mv1_done"], 1)
            prep_norm(0, 1, None)
            def matrices_rest(j):
                dve.wait_ge(S["ab_hi_done"], j + 1)
                v.tensor_tensor(ab_lo[:, 2 * j:2 * j + 2].rearrange("p h m c -> p h (m c)"), psAB[j % 2],
                                ab_hi[:, 2 * j:2 * j + 2].rearrange("p h m c -> p h (m c)").bitcast(F32),
                                ALU.subtract).then_inc(S["ab_split"], 1)

            matrices_rest(0)
            matrices_rest(1)
            prep_turned(0, 1)
            def slot(g0, b0, s, live, live_b):
                misc(g0, b0, s, live, live_b)
                route(b0, s, live_b, 0)
                if live(2):
                    p2 = (s - 2) % 4
                    dve.wait_ge(S["probs_ready"], 2 * (g0 + s - 1))
                    v.reciprocal(rinv[:, p2].rearrange("p h q -> p (h q)"),
                                 rsum[:, p2].rearrange("p h q -> p (h q)")).then_inc(S["rinv_ready"], 1)
                route(b0, s, live_b, 1)
                misc_stats(b0, s, live_b)
                if live(0):
                    dve.wait_ge(S["t_hi_done"], g0 + s + 1)
                    v.tensor_tensor(t_lo[:, s % 2], psT[:], t_hi[:, s % 2].bitcast(F32),
                                    ALU.subtract).then_inc(S["t_split"], 1)
                route(b0, s, live_b, 2)

                if setup_slot(s, live):
                    matrices_rest(2 * s + 2)
                    matrices_rest(2 * s + 3)
                def score_max(h):
                    p1 = (s - 1) % 4
                    wait_apart(dve, S["s_ready"], 2 * (g0 + s - 1) + 1 + h)
                    for q, (a, z) in enumerate(((0, P), (P, 384))):
                        last = v.tensor_tensor_reduce(nscore[:, h, a:z], psS[:, h, a:z], mask[:, a:z],
                                                      -1.0, -MASKED, ALU.add, ALU.min, nmax[:, p1, h, q:q + 1])
                    last.then_inc(S["nmax_ready"], 1)

                if live(1):
                    score_max(0)
                route(b0, s, live_b, 3)
                route(b0, s, live_b, 4)
                if live(3):
                    dve.wait_ge(S["p_hi_done"], g0 + s - 2)
                    v.tensor_tensor(p_lo[:, (s - 3) % 2], psP[:, :, 0:384], p_hi[:, (s - 3) % 2].bitcast(F32),
                                    ALU.subtract).then_inc(S["p_split"], 1)
                if live(1):
                    score_max(1)
                if live(4):
                    dve.wait_ge(S["z_hi_done"], g0 + s - 3)
                    v.tensor_tensor(z_lo[:, (s - 4) % 2], psZ[:], z_hi[:, (s - 4) % 2].bitcast(F32),
                                    ALU.subtract).then_inc(S["z_split"], 1)

            def route(b0, s, live_b, k):
                r, db = s % PAIRS, s // PAIRS
                if r not in (4, 5) or not live_b(2):
                    return
                n = b0 + db - 2
                rank_e = rev_e[:].unsqueeze(1).broadcast_to([P, 2, E])
                scv = psM[:, 0:2 * E].rearrange("p (t e) -> p t e", t=2)
                over = lambda a: a.unsqueeze(2).broadcast_to([P, 2, E])
                best = pay[:, db, :, C_SCORE]
                if r == 4:
                    if k == 0:
                        dve.wait_ge(S["scored"], n + 1)
                        v.tensor_reduce(best, scv, AX.X, ALU.max).then_inc(S["argmax_steps"], 1)
                    elif k == 1:
                        dve.wait_ge(S["argmax_steps"], 4 * n + 1)
                        v.tensor_tensor(hits[:], scv, over(best), ALU.is_ge).then_inc(S["argmax_steps"], 1)
                    elif k == 2:
                        dve.wait_ge(S["argmax_steps"], 4 * n + 2)
                        v.tensor_tensor(hitr[:], hits[:], rank_e, ALU.mult).then_inc(S["argmax_steps"], 1)
                    elif k == 3:
                        dve.wait_ge(S["argmax_steps"], 4 * n + 3)
                        v.tensor_reduce(first[:], hitr[:], AX.X, ALU.max).then_inc(S["argmax_steps"], 1)
                    elif k == 4:
                        dve.wait_ge(S["argmax_steps"], 4 * n + 4)
                        v.tensor_tensor(oh[:], rank_e, over(first[:]), ALU.is_equal).then_inc(S["onehot_ready"], 1)
                else:
                    if k == 4 and db == 0 and not live_b(0):
                        dve.wait_ge(S["dest_steps"], 3 * n + 3)
                        v.tensor_copy(ends[:], base[:, 1 - db, :]).then_inc(S["ends_ready"], 1)
                    if k == 0:
                        dve.wait_ge(S["ranked"], n + 1)
                        v.tensor_tensor(dsum[:], scv, base[:, db, :].unsqueeze(1).broadcast_to([P, 2, E]), ALU.add)
                        v.tensor_tensor(base[:, 1 - db, :], psM[:, 2 * E:3 * E], base[:, db, :],
                                        ALU.add).then_inc(S["dest_steps"], 1)
                    elif k == 1:
                        dve.wait_ge(S["dest_steps"], 3 * n + 1)
                        v.tensor_tensor(dsel[:], dsum[:], oh[:], ALU.mult).then_inc(S["dest_steps"], 1)
                    elif k == 2:
                        dve.wait_ge(S["dest_steps"], 3 * n + 2)
                        v.tensor_reduce(dstf[:], dsel[:], AX.X, ALU.add).then_inc(S["dest_steps"], 1)
                    elif k == 3:
                        dve.wait_ge(S["dest_steps"], 3 * n + 3)
                        v.tensor_copy(dst[:, db, :], dstf[:]).then_inc(S["dest_ready"], 1)

            def misc_stats(b0, s, live_b):
                r, db = s % PAIRS, s // PAIRS
                if r == 1 and live_b(2):
                    aggregate(st3, mv3, S["st3_done"], S["mv3_done"], b0 + db - 1)
                if r == 2 and live_b(-1):
                    aggregate(st1, mv1, S["st1_done"], S["mv1_done"], b0 + db + 2)
                if r == 7 and live_b(1):
                    aggregate(st2, mv2, S["st2_done"], S["mv2_done"], b0 + db)

            def misc(g0, b0, s, live, live_b):
                r, db = s % PAIRS, s // PAIRS
                if r == 0 and live_b(2):
                    n = b0 + db - 1
                    dve.wait_ge(S["rs2_done"], n)
                    normalise(lambda t: an[:, t, :], lambda t: psM[:, t * P:(t + 1) * P], mv2,
                              lambda t: rs2[:, t:t + 1], S["a_norm"])
                if not live(0) and s == 9:
                    dve.wait_ge(S["bias_done"], E // 2 + 1)
                    b1v = wx[:, :, B1:W2]
                    v.tensor_tensor(b1v, psT[:, 0, 0:E * FB].rearrange("p (e j) -> p e j", e=E), b1v,
                                    ALU.add).then_inc(S["bias_added"], 1)
                if r == 1 and live_b(2):
                    n = b0 + db - 1
                    dve.wait_ge(S["x1_ready"], n)
                    stats(lambda t: pay[:, db, t, 0:P], st3, S["st3_done"])
                if r == 2 and live_b(2):
                    n = b0 + db - 1
                    dve.wait_ge(S["r3_steps"], 6 * n - 4)
                    normalise(lambda t: fn[:, t, :], lambda t: pay[:, db, t, 0:P], mv3,
                              lambda t: pay[:, db, t, C_RSTD:C_RSTD + 1], S["f_ready"])
                if r == 2 and live_b(-1):
                    prep_stats((db + 1) % 2, b0 + db + 2)
                if r == 3 and live_b(2):
                    v.scalar_tensor_tensor(pay[:, db, :, C_SHIFT], mv3[:, :, 0], -1.0, pay[:, db, :, C_RSTD],
                                           ALU.mult, ALU.mult)
                    v.tensor_copy(pay[:, db, :, C_ID].bitcast(U32), idf[:, db, :])
                    v.tensor_scalar(idf[:, 1 - db, :], idf[:, db, :], float(T), None, ALU.add)
                if r == 3 and live_b(-1):
                    prep_norm((db + 1) % 2, b0 + db + 2, b0 + db + 1)
                if r == 6 and live_b(-1):
                    prep_turned((db + 1) % 2, b0 + db + 2)
                if r == 7 and live_b(1):
                    n = b0 + db
                    dve.wait_ge(S["a_tr"], n)
                    stats(lambda t: psM[:, t * P:(t + 1) * P], st2, S["st2_done"])

            dve.wait_ge(S["consts_ready"], 1)
            phases(dve, slot)
            FFN["dve"](dve)

        @block.gpsimd
        def _(pool):
            g = nc.gpsimd

            def inv_sqrt(dst_, ve, src, mv_done, ve_done, done, n):
                pool.wait_ge(mv_done, n)
                g.tensor_tensor(ve[:], src, eps_t[:], ALU.add).then_inc(ve_done, 1)
                pool.wait_ge(ve_done, n)
                g.tensor_tensor(dst_, ve[:], neg_half[:], ALU.pow).then_inc(done, 1)

            def prep_split(par, n):
                wait_apart(pool, S["xn_ready"], n)
                g.tensor_copy(xk_hi[:, par], xn[:]).then_inc(S["xk_hi_done"], 1)
                pool.wait_ge(S["xk_hi_done"], n)
                g.tensor_tensor(xk_lo[:, par], xn[:], xk_hi[:, par].bitcast(F32),
                                ALU.subtract).then_inc(S["xk_split"], 1)

            steps = ctx.enter_context(nc.semaphore("const_steps"))
            nst = [0]

            def step(ins):
                nst[0] += 1
                ins.then_inc(steps, 1)
                pool.wait_ge(steps, nst[0])

            step(g.memset(neg_half[:], -0.5))
            step(g.memset(eps_t[:], EPS))
            inv_sqrt(rs1[:], ve1, mv1[:, :, 1], S["mv1_done"], S["ve1_done"], S["rs1_done"], 1)
            step(g.memset(ident[:], 0.0))
            step(g.affine_select(ident[:], ident[:], [[-1, P]], ALU.not_equal, 1.0, base=0, channel_multiplier=1))
            step(g.memset(onesb[:], 1.0))
            step(g.memset(mask[:], 0.0))
            for a in (0, T):
                step(g.affine_select(mask[:, a:a + P], mask[:, a:a + P], [[-1, P]], ALU.is_ge, MASKED, base=0,
                                     channel_multiplier=1))
            step(g.affine_select(before[:], onesb[:], [[1, P]], ALU.is_gt, 0.0, base=0, channel_multiplier=-1))
            step(g.iota(iota_i[:], [[-1, E]], base=E, channel_multiplier=0))
            step(g.tensor_copy(rev_e[:], iota_i[:]))
            step(g.iota(iota_i[:], [[REGION, E]], base=0, channel_multiplier=0))
            step(g.tensor_copy(base[:, 0, :], iota_i[:]))
            step(g.tensor_copy(regb[:], iota_i[:]))
            step(g.iota(tixi[:], [[1, TILES]], base=0, channel_multiplier=0))
            step(g.tensor_copy(tix[:], tixi[:]))
            step(g.memset(padr[:], 0.0))
            g.memset(padr[:, :, C_ID:C_ID + 1].bitcast(U32), NOWHERE).then_inc(S["pads_ready"], 1)
            step(g.iota(iota_i[:, 0:2], [[P, 2]], base=0, channel_multiplier=1))
            g.tensor_copy(idf[:, 0, :], iota_i[:, 0:2]).then_inc(S["consts_ready"], 1)

            prep_split(0, 1)

            def slot(g0, b0, s, live, live_b):
                r, db = s % PAIRS, s // PAIRS
                if live(2):
                    p2 = (s - 2) % 4
                    pool.wait_ge(S["rinv_ready"], g0 + s - 1)
                    for q, (a, z) in enumerate(((0, P), (P, 384))):
                        pr = prob[:, p2, :, a:z]
                        last = g.tensor_tensor(pr, pr, rinv[:, p2, :, q:q + 1].broadcast_to([P, 2, z - a]), ALU.mult)
                    last.then_inc(S["norm_ready"], 1)
                if r == 0 and live_b(2):
                    n = b0 + db - 1
                    pool.wait_ge(S["a_norm"], n)
                    pool.wait_ge(S["xr_loaded"], 16 * n)
                    g.tensor_tensor(pay[:, db, :, 0:P], an[:], xres[:, db], ALU.add).then_inc(S["x1_ready"], 1)
                if r == 1 and live_b(2):
                    n = b0 + db - 2
                    k = [6 * n]

                    def link(ins):
                        k[0] = k[0] + 1
                        ins.then_inc(S["r3_steps"], 1)
                        pool.wait_ge(S["r3_steps"], k[0])

                    rs3 = pay[:, db, :, C_RSTD]
                    pool.wait_ge(S["mv3_done"], n + 1)
                    link(g.tensor_tensor(ve3[:], mv3[:, :, 1], eps_t[:], ALU.add))
                    link(g.tensor_tensor(rs3, ve3[:], neg_half[:], ALU.pow))
                    link(g.tensor_tensor(w3[:, 0, :], mv3[:, :, 1], rs3, ALU.mult))
                    link(g.tensor_tensor(w3[:, 1, :], w3[:, 0, :], rs3, ALU.mult))
                    link(g.tensor_tensor(w3[:, 2, :], w3[:, 1, :], eps_t[:], ALU.add))
                    link(g.tensor_tensor(pay[:, db, :, C_RSTD2], w3[:, 2, :], neg_half[:], ALU.pow))
                if r == 2 and live_b(-1):
                    inv_sqrt(rs1[:], ve1, mv1[:, :, 1], S["mv1_done"], S["ve1_done"], S["rs1_done"], b0 + db + 2)
                if r == 4 and live_b(-1):
                    if live_b(1):
                        wait_apart(pool, S["z_ready"], PAIRS * (b0 + db))
                    prep_split((db + 1) % 2, b0 + db + 2)
                if r == 5 and live_b(2):
                    if not live(0) and db == 1:
                        pool.wait_ge(S["pad_stored"], 16 * E)
                    wait_apart(pool, S["dest_ready"], b0 + db - 1)
                    for t in range(2):
                        g.indirect_dma_start(rows, bass.IndirectOffsetOnAxis(ap=dst[:, db, t:t + 1], axis=0),
                                             pay[:, db, t, :], None).then_inc(S["scattered"], 16)
                if r == 7 and live_b(1):
                    inv_sqrt(rs2[:], ve2, mv2[:, :, 1], S["mv2_done"], S["ve2_done"], S["rs2_done"], b0 + db)
                if r == 7 and live_b(2):
                    pool.wait_ge(S["scattered"], 32 * (b0 + db - 1))

            phases(pool, slot)
            FFN["pool"](pool)


def kernel(L0_attn_x, L0_attn_w_kv_down, L0_attn_w_kv_up, L0_attn_w_q, L0_attn_w_out, L0_ffn_centroids,
           L0_ffn_gamma, L0_ffn_beta, L0_ffn_W1, L0_ffn_b1, L0_ffn_W2, L0_ffn_b2):
    import numpy as np
    import concourse.bacc as bacc
    from concourse.bass_utils import run_bass_kernel_spmd

    shape = L0_attn_x.shape
    C = shape[-1]
    HD = L0_attn_w_q.shape[1]
    E, F, _ = L0_ffn_W1.shape
    lay = lambda a, *perm: np.ascontiguousarray(np.transpose(a, perm))
    arrays = {
        "x": np.asarray(L0_attn_x).reshape(-1, C),
        "wd_t": lay(L0_attn_w_kv_down, 1, 0),
        "wup": np.asarray(L0_attn_w_kv_up),
        "wq_t": lay(np.asarray(L0_attn_w_q).reshape(C, HD // P, P), 2, 1, 0),
        "wo": lay(np.asarray(L0_attn_w_out).reshape(HD // P, P, C), 1, 0, 2),
        "cent_t": lay(L0_ffn_centroids, 1, 0),
        "gamma_t": lay(L0_ffn_gamma, 1, 0),
        "beta_t": lay(L0_ffn_beta, 1, 0),
        "ffn_w": np.concatenate([
            lay(L0_ffn_W1, 2, 0, 1),
            lay(np.asarray(L0_ffn_b1).reshape(E, F // P, P), 2, 0, 1),
            lay(np.asarray(L0_ffn_W2).reshape(E, C, F // P, P), 3, 0, 2, 1).reshape(P, E, F),
            lay(L0_ffn_b2, 1, 0).reshape(C, E, 1)], axis=2),
    }
    arrays = {k: np.ascontiguousarray(a) for k, a in arrays.items()}
    nc = bacc.Bacc("TRN2", target_bir_lowering=False, num_devices=1)
    args = [nc.dram_tensor(k, a.shape, mybir.dt.from_np(a.dtype), kind="ExternalInput").ap()
            for k, a in arrays.items()]
    out = nc.dram_tensor("out", arrays["x"].shape, F32, kind="ExternalOutput").ap()
    block_kernel(nc, *args, out)
    r = run_bass_kernel_spmd(nc, [arrays], core_ids=[0])
    return r.results[0]["out"].reshape(shape)
```
